# Optimizing a Trainium2 kernel written in Bass

```python
import numpy as np
import jax
import jax.numpy as jnp

def _softmax(x, axis=-1):
    return jax.nn.softmax(x, axis=axis)

def _gelu(x):
    return jax.nn.gelu(x, approximate=True)

def _silu(x):
    return jax.nn.silu(x)

def _sigmoid(x):
    return jax.nn.sigmoid(x)

def _layernorm(x, axis=-1, eps=1e-05):
    m = jnp.mean(x, axis=axis, keepdims=True)
    v = jnp.var(x, axis=axis, keepdims=True)
    return (x - m) / jnp.sqrt(v + eps)

def _scatter_add(tgt, idx, src, axis=0):
    return tgt.at[idx].add(src)

def _segment_sum(src, seg, n):
    return jax.ops.segment_sum(src, seg, n)
kernel_name = 'mk_hybrid_d1_jaxref_r8_d00e9f'

def setup_inputs(seed: int=0):
    np.random.seed(seed)
    _w = jnp.asarray

    def _L0_attn_a_setup():
        import jax, jax.numpy as jnp
        import numpy as np
        from math import sqrt
        N_HEAD = 16
        W_SCALE = 0.02

        def _reference_tuple_inner(x, W_dq, W_uq, W_dkv, W_uk, W_uv, W_o):
            B, T, C = x.shape
            nh = N_HEAD
            hs = C // nh
            n_kvl = W_dkv.shape[0]
            k_eff = (W_dq.T @ W_uq.T @ W_uk).reshape(nh, hs, n_kvl)
            v_eff = jnp.transpose((W_uv.T @ W_o.T).reshape(n_kvl, nh, hs), (1, 0, 2))
            c_kv = x @ W_dkv.T
            q = x @ W_dq.T @ W_uq.T
            q = q.reshape(B, T, nh, hs)
            q_lat = jnp.einsum('bqhd,hdl->bhql', q, k_eff)
            attn = jnp.einsum('bhql,bkl->bhqk', q_lat, c_kv) / sqrt(hs)
            causal = jnp.tril(jnp.ones((T, T), dtype=bool))
            attn = jnp.where(causal[None, None], attn, -jnp.inf)
            attn = jax.nn.softmax(attn, axis=-1)
            y_lat = jnp.einsum('bhqk,bkl->bhql', attn, c_kv)
            y = jnp.einsum('bhql,hld->bqhd', y_lat, v_eff).reshape(B, T, C)
            return (y, c_kv)
        key = jax.random.key(seed)
        ks = jax.random.split(key, 7)
        B, T, C = (2, 256, 128)
        QL, KVL = (64, 64)
        return {'x': jax.random.normal(ks[0], (B, T, C), dtype=jnp.float32), 'W_dq': jax.random.normal(ks[1], (QL, C), dtype=jnp.float32) * W_SCALE, 'W_uq': jax.random.normal(ks[2], (C, QL), dtype=jnp.float32) * W_SCALE, 'W_dkv': jax.random.normal(ks[3], (KVL, C), dtype=jnp.float32) * W_SCALE, 'W_uk': jax.random.normal(ks[4], (C, KVL), dtype=jnp.float32) * W_SCALE, 'W_uv': jax.random.normal(ks[5], (C, KVL), dtype=jnp.float32) * W_SCALE, 'W_o': jax.random.normal(ks[6], (C, C), dtype=jnp.float32) * W_SCALE}
    _L0_attn_a_in = _L0_attn_a_setup()

    def _L0_attn_b_setup():
        import jax, jax.numpy as jnp
        import numpy as np
        HEADS = 16
        SCALE = 8.0
        EPS = 1e-12

        def _l2norm(t):
            n = jnp.sqrt(jnp.sum(t * t, axis=-1, keepdims=True))
            return t / jnp.maximum(n, EPS)
        key = jax.random.key(seed)
        k0, k1, k2, k3, k4 = jax.random.split(key, 5)
        b, n, d = (1, 512, 128)
        w_scale = 1.0 / np.sqrt(d)
        return {'x': jax.random.normal(k0, (b, n, d), dtype=jnp.float32), 'Wq': jax.random.normal(k1, (d, d), dtype=jnp.float32) * w_scale, 'Wk': jax.random.normal(k2, (d, d), dtype=jnp.float32) * w_scale, 'Wv': jax.random.normal(k3, (d, d), dtype=jnp.float32) * w_scale, 'Wo': jax.random.normal(k4, (d, d), dtype=jnp.float32) * w_scale}
    _L0_attn_b_in = _L0_attn_b_setup()

    def _L0_ffn_setup():
        import jax, jax.numpy as jnp
        import numpy as np
        DIM = 128

        def _reference_tuple_inner(x, W_r, W_k, W_v, mu_r, mu_k):
            B, T, C = x.shape
            x_prev = jnp.concatenate([jnp.zeros((B, 1, C), x.dtype), x[:, :-1, :]], axis=1)
            xr = mu_r * x + (1.0 - mu_r) * x_prev
            xk = mu_k * x + (1.0 - mu_k) * x_prev
            r = jax.nn.sigmoid(jnp.einsum('btc,dc->btd', xr, W_r))
            k = jnp.einsum('btc,dc->btd', xk, W_k)
            k_act = jnp.square(jax.nn.relu(k))
            out = r * jnp.einsum('btc,dc->btd', k_act, W_v)
            new_state = x[:, -1, :]
            return (out, new_state)
        key = jax.random.key(seed)
        ks = jax.random.split(key, 6)
        B, T, C = (8, 256, DIM)
        x = jax.random.normal(ks[0], (B, T, C), dtype=jnp.float32)
        s = 1.0 / np.sqrt(C)
        W_r = jax.random.uniform(ks[1], (C, C), jnp.float32, -s, s)
        W_k = jax.random.uniform(ks[2], (C, C), jnp.float32, -s, s)
        W_v = jax.random.uniform(ks[3], (C, C), jnp.float32, -s, s)
        mu_r = jax.random.uniform(ks[4], (C,), jnp.float32)
        mu_k = jax.random.uniform(ks[5], (C,), jnp.float32)
        return {'x': x, 'W_r': W_r, 'W_k': W_k, 'W_v': W_v, 'mu_r': mu_r, 'mu_k': mu_k}
    _L0_ffn_in = _L0_ffn_setup()
    _d = {'L0_attn_a_x': _L0_attn_a_in['x'], 'L0_attn_a_W_dq': _L0_attn_a_in['W_dq'], 'L0_attn_a_W_uq': _L0_attn_a_in['W_uq'], 'L0_attn_a_W_dkv': _L0_attn_a_in['W_dkv'], 'L0_attn_a_W_uk': _L0_attn_a_in['W_uk'], 'L0_attn_a_W_uv': _L0_attn_a_in['W_uv'], 'L0_attn_a_W_o': _L0_attn_a_in['W_o'], 'L0_attn_b_Wq': _L0_attn_b_in['Wq'], 'L0_attn_b_Wk': _L0_attn_b_in['Wk'], 'L0_attn_b_Wv': _L0_attn_b_in['Wv'], 'L0_attn_b_Wo': _L0_attn_b_in['Wo'], 'L0_ffn_W_r': _L0_ffn_in['W_r'], 'L0_ffn_W_k': _L0_ffn_in['W_k'], 'L0_ffn_W_v': _L0_ffn_in['W_v'], 'L0_ffn_mu_r': _L0_ffn_in['mu_r'], 'L0_ffn_mu_k': _L0_ffn_in['mu_k']}
    _x0 = _d['L0_attn_a_x']
    _d['L0_attn_a_x'] = jax.random.normal(jax.random.fold_in(jax.random.key(seed), 1), (16, 512, 128), dtype=_x0.dtype)
    del _x0
    return _d

def reference(L0_attn_a_x, L0_attn_a_W_dq, L0_attn_a_W_uq, L0_attn_a_W_dkv, L0_attn_a_W_uk, L0_attn_a_W_uv, L0_attn_a_W_o, L0_attn_b_Wq, L0_attn_b_Wk, L0_attn_b_Wv, L0_attn_b_Wo, L0_ffn_W_r, L0_ffn_W_k, L0_ffn_W_v, L0_ffn_mu_r, L0_ffn_mu_k):

    def _L0_attn_a_ref(x, W_dq, W_uq, W_dkv, W_uk, W_uv, W_o):
        import jax, jax.numpy as jnp
        import numpy as np
        from math import sqrt
        N_HEAD = 16
        W_SCALE = 0.02

        def _reference_tuple_inner(x, W_dq, W_uq, W_dkv, W_uk, W_uv, W_o):
            B, T, C = x.shape
            nh = N_HEAD
            hs = C // nh
            n_kvl = W_dkv.shape[0]
            k_eff = (W_dq.T @ W_uq.T @ W_uk).reshape(nh, hs, n_kvl)
            v_eff = jnp.transpose((W_uv.T @ W_o.T).reshape(n_kvl, nh, hs), (1, 0, 2))
            c_kv = x @ W_dkv.T
            q = x @ W_dq.T @ W_uq.T
            q = q.reshape(B, T, nh, hs)
            q_lat = jnp.einsum('bqhd,hdl->bhql', q, k_eff)
            attn = jnp.einsum('bhql,bkl->bhqk', q_lat, c_kv) / sqrt(hs)
            causal = jnp.tril(jnp.ones((T, T), dtype=bool))
            attn = jnp.where(causal[None, None], attn, -jnp.inf)
            attn = jax.nn.softmax(attn, axis=-1)
            y_lat = jnp.einsum('bhqk,bkl->bhql', attn, c_kv)
            y = jnp.einsum('bhql,hld->bqhd', y_lat, v_eff).reshape(B, T, C)
            return (y, c_kv)
        return _reference_tuple_inner(x, W_dq, W_uq, W_dkv, W_uk, W_uv, W_o)[0]

    def _L0_attn_b_ref(x, Wq, Wk, Wv, Wo):
        import jax, jax.numpy as jnp
        import numpy as np
        HEADS = 16
        SCALE = 8.0
        EPS = 1e-12

        def _l2norm(t):
            n = jnp.sqrt(jnp.sum(t * t, axis=-1, keepdims=True))
            return t / jnp.maximum(n, EPS)
        b, n, d = x.shape
        h = HEADS
        dh = d // h

        def proj(W):
            y = jnp.einsum('bnd,df->bnf', x, W)
            return y.reshape(b, n, h, dh).transpose(0, 2, 1, 3)
        q, k, v = (proj(Wq), proj(Wk), proj(Wv))
        q = _l2norm(q)
        k = _l2norm(k)
        sim = jnp.einsum('bhid,bhjd->bhij', q, k) * SCALE
        mask_value = -jnp.finfo(sim.dtype).max
        causal = jnp.triu(jnp.ones((n, n), dtype=bool), 1)
        sim = jnp.where(causal, mask_value, sim)
        attn = jax.nn.softmax(sim, axis=-1)
        o = jnp.einsum('bhij,bhjd->bhid', attn, v)
        o = o.transpose(0, 2, 1, 3).reshape(b, n, d)
        return jnp.einsum('bnf,fd->bnd', o, Wo)

    def _L0_ffn_ref(x, W_r, W_k, W_v, mu_r, mu_k):
        import jax, jax.numpy as jnp
        import numpy as np
        DIM = 128

        def _reference_tuple_inner(x, W_r, W_k, W_v, mu_r, mu_k):
            B, T, C = x.shape
            x_prev = jnp.concatenate([jnp.zeros((B, 1, C), x.dtype), x[:, :-1, :]], axis=1)
            xr = mu_r * x + (1.0 - mu_r) * x_prev
            xk = mu_k * x + (1.0 - mu_k) * x_prev
            r = jax.nn.sigmoid(jnp.einsum('btc,dc->btd', xr, W_r))
            k = jnp.einsum('btc,dc->btd', xk, W_k)
            k_act = jnp.square(jax.nn.relu(k))
            out = r * jnp.einsum('btc,dc->btd', k_act, W_v)
            new_state = x[:, -1, :]
            return (out, new_state)
        return _reference_tuple_inner(x, W_r, W_k, W_v, mu_r, mu_k)[0]
    x = L0_attn_a_x
    x = x + _L0_attn_a_ref(_layernorm(x, axis=-1), L0_attn_a_W_dq, L0_attn_a_W_uq, L0_attn_a_W_dkv, L0_attn_a_W_uk, L0_attn_a_W_uv, L0_attn_a_W_o)
    x = x + _L0_ffn_ref(_layernorm(x, axis=-1), L0_ffn_W_r, L0_ffn_W_k, L0_ffn_W_v, L0_ffn_mu_r, L0_ffn_mu_k)
    x = x + _L0_attn_b_ref(_layernorm(x, axis=-1), L0_attn_b_Wq, L0_attn_b_Wk, L0_attn_b_Wv, L0_attn_b_Wo)
    x = x + _L0_ffn_ref(_layernorm(x, axis=-1), L0_ffn_W_r, L0_ffn_W_k, L0_ffn_W_v, L0_ffn_mu_r, L0_ffn_mu_k)
    return x

_drawn_inputs = setup_inputs


def setup_inputs(seed=0):
    import zlib

    import numpy as np

    out = dict(_drawn_inputs(seed))
    spreads = {}
    factors = {'L0_attn_a_W_dq': 8.0,
     'L0_attn_a_W_uq': 8.0,
     'L0_attn_a_W_dkv': 8.0,
     'L0_attn_a_W_uk': 8.0,
     'L0_attn_a_W_uv': 8.0,
     'L0_attn_a_W_o': 8.0,
     'L0_ffn_mu_r': 14.71,
     'L0_ffn_W_r': 2.954}
    for name, (base, spread) in spreads.items():
        noise = np.random.default_rng([zlib.crc32(name.encode()), seed]).standard_normal(out[name].shape)
        drawn = base * np.exp(spread * noise) if base else spread * noise
        out[name] = jnp.asarray(drawn.astype(out[name].dtype))
    for name, factor in factors.items():
        out[name] = (out[name] * factor).astype(out[name].dtype)
    return out
```

```python
import numpy as np
import concourse.bass as bass
from concourse import mybir
from contextlib import ExitStack

F32, BF16 = mybir.dt.float32, mybir.dt.bfloat16
ALU, ACT, AX = mybir.AluOpType, mybir.ActivationFunctionType, mybir.AxisListType

P = 128
HEADS = 16
PAIRS = HEADS // 2
GROUP = 4
GROUPS = PAIRS // GROUP
BLK = 64
BANK = 512
ROWS = 48
BIG = -3.0e38
EPS = 1e-5
STACK = [(0, (0, 0, 0), (0, 1, 2)), (3, (1, 1), (0, 1)), (5, (2,), (0,))]
PRODUCTS = 6


class Lane:

    def __init__(self, sem, by=1):
        self.sem, self.by, self.count, self.items, self.seen = sem, by, 0, [], {}

    def mark(self):
        self.count += self.by
        return (self, self.count)


class Program:

    def __init__(self, engines, dmas):
        self.lanes, self.dmas, self.marks = engines, dmas, {}

    def put(self, lane, make, wait=(), done=None, dma=None, first=None):
        line, waits = self.lanes[lane], []
        for name in wait:
            m = self.marks.get(name)
            if m and line.seen.get(m[0], 0) < m[1]:
                line.seen[m[0]] = m[1]
                waits.append(m)
        inc = None
        if done is not None:
            source = self.dmas[dma] if dma else line
            self.marks[done] = source.mark()
            inc = (source.sem, source.by)
        line.items.append((waits, make, inc, first))

    def cut(self):
        piece = {k: v.items for k, v in self.lanes.items()}
        for v in self.lanes.values():
            v.items, v.seen = [], {}
        return piece

    def counts(self):
        return {x: x.count for x in [*self.lanes.values(), *self.dmas.values()]}


def emit(engine, items, i=0, grow=None):
    for waits, make, inc, first in items:
        arg = first(engine, i) if first else i
        values = [i * grow[source] + value if grow else value for source, value in waits]
        for value in values if grow else ():
            engine.compute_val(value)
        for (source, _), value in zip(waits, values):
            engine.wait_ge(source.sem, value)
        made = make(engine, arg)
        if inc:
            made.then_inc(*inc)


def tiles_of_keys():
    n = BANK // BLK
    return [[(0, 0)]] + [[(i, 0), (n - i, BANK - BLK * i)] for i in range(1, n // 2)] + [[(n // 2, 0)]]


def build(nc, x, wdq, wuq, wdkv, wuk, wuv, wo_a, wq, wk, wv, wo_b, wr, wkf, wvf, mur, muk, out):
    B, T, C = x.shape
    NT = T // P
    NB = T // BLK
    D = C // HEADS
    QL, KVL = wdq.shape[0], wdkv.shape[0]
    NPROB = 4

    ctx = ExitStack()
    with ctx:
        def sb(name, shape, dt=F32):
            return ctx.enter_context(nc.sbuf_tensor(name, shape, dt))

        def sem(name):
            return ctx.enter_context(nc.semaphore(name))

        ident = sb("ident", [P, P])
        ident_b = sb("ident_b", [P, P], BF16)
        ones_b = sb("ones_b", [3, PAIRS * BLK], BF16)
        last_stats = sb("last_stats", [P, 6])
        mask = sb("mask", [P, BLK], BF16)
        mask_t = sb("mask_t", [P, BLK], BF16)
        seen = sb("seen", [P, BLK])
        minus_half = sb("minus_half", [P, 1])
        w_in = {n: sb("raw_" + n, list(a.shape)) for n, a in
                dict(dq=wdq, uq=wuq, dkv=wdkv, uk=wuk, uv=wuv, o=wo_a, r=wr, k=wkf, v=wvf).items()}
        w_qk = sb("w_qk", [P, 2, C])
        w_v = sb("w_v", [P, C])
        w_ob = sb("w_ob", [P, C])
        mu = sb("mu", [P, 2])
        T_uq = sb("T_uq", [QL, C])
        T_o = sb("T_o", [P, C])
        T_r = sb("T_r", [P, C])
        T_k = sb("T_k", [P, C])
        T_v = sb("T_v", [P, C])
        M_q = sb("M_q", [P, C])
        M_qT = sb("M_qT", [P, C])
        k_effT = sb("k_effT", [KVL, C])
        v_eff = sb("v_eff", [KVL, C])
        M_k = sb("M_k", [P, C])
        M_v = sb("M_v", [P, C])
        xs = {n: sb("x_" + n, [P, NT, C]) for n in ("in", "a", "ffn", "b", "out")}
        stats = {n: sb(f"stats_{n}", [P, NT, 6]) for n in ("1", "2", "3", "4")}
        mv = {n: sb(f"mv_{n}", [P, NT, 2]) for n in stats}
        rstd = {n: sb(f"rstd_{n}", [P, NT]) for n in stats}
        xn = {n: sb(f"xn_{n}", [P, NT, C]) for n in stats}
        xnT = {n: sb(f"xnT_{n}", [P, T + 1]) for n in stats}
        ffn = {n: {b: sb(f"{b}_{n}", [P, T]) for b in ("diff", "xr", "xk", "act", "gate")}
               for n in ("2", "4")}
        parts = {n: sb("parts_" + n, [P, 3, T], BF16) for n in "qk"}
        rest = {n: sb("rest_" + n, [P, T]) for n in parts}
        stack = {n: sb("stack_" + n, [P, PAIRS, T], BF16) for n in ("qa", "qb", "k")}
        diag = {n: sb("diag_" + n, [P, PAIRS, NB, P], BF16) for n in ("qa", "ka", "kb")}
        vals = {n: sb("vals_" + n, [P, NB, PAIRS, 32]) for n in "ab"}
        rowmax = sb("rowmax", [P, P])
        mparts = sb("mparts", [PAIRS * NB, 3, P], BF16)
        mrest = sb("mrest", [PAIRS * NB, P])
        prob = [sb(f"prob{i}", [P, 2, BANK]) for i in range(NPROB)]
        outT = {n: [sb(f"outT_{n}{g}", [P, T]) for g in range(GROUPS)] for n in "ab"}
        rden = {n: [sb(f"rden_{n}{g}", [P, NT * 2 * GROUP]) for g in range(GROUPS)] for n in "ab"}
        y = {n: sb("y_" + n, [P, NT, C]) for n in "ab"}
        yT = sb("yT", [P, T])
        qk = sb("qk", [P, NT, 2, C])
        ssum = sb("ssum", [P, NT, 2 * HEADS])
        rnorm = sb("rnorm", [P, NT, 2 * HEADS])

        def pb(name, shape, dt=F32):
            return ctx.enter_context(nc.psum_tensor(name, shape, dt))

        score = [pb(f"score{i}", [P, 2, BANK]) for i in range(2)]
        acc = pb("acc", [P, BANK])
        misc = [pb(f"misc{i}", [P, BANK]) for i in range(3)]

        scratch = {n: nc.dram_tensor("scratch_" + n, (PRODUCTS, P, T), BF16, kind="Internal").ap() for n in parts}

        lanes = {n: Lane(sem("s_" + n)) for n in ("pe", "act", "dve", "pool", "sp")}
        dmas = {n: Lane(sem("s_dma_" + n), 16) for n in
                ["w", "x", "out", "max", "ones"] + ["scr_" + n for n in parts] + ["stk_" + n for n in stack]}
        pg = Program(lanes, dmas)
        put = pg.put

        def alone(make, wait, done):
            put("pool", make, wait=["pool before", *wait], done=done)
            pg.marks["pool before"] = pg.marks[done]

        ring = [0]

        def bank():
            k = ring[0] % 3
            ring[0] += 1
            return misc[k], f"misc{k} read"

        def setup():
            loads = [(w_in["dq"], wdq), (w_in["uq"], wuq), (w_in["dkv"], wdkv), (w_in["uk"], wuk),
                     (w_in["uv"], wuv), (w_in["o"], wo_a), (w_in["r"], wr), (w_in["k"], wkf), (w_in["v"], wvf)]
            for dst, src in loads:
                put("sp", lambda e, i, d=dst, s=src: e.dma_start(d[:, :], s), done="weights", dma="w")
            for dst, src in [(w_qk[:, 0, :], wq), (w_qk[:, 1, :], wk), (w_v[:, :], wv), (w_ob[:, :], wo_b),
                             (mu[:, 0:1], mur.rearrange("(c o) -> c o", o=1)),
                             (mu[:, 1:2], muk.rearrange("(c o) -> c o", o=1))]:
                put("sp", lambda e, i, d=dst, s=src: e.dma_start(d, s), done="weights", dma="w")
            for m in (ident, ident_b):
                alone(lambda e, i, m=m: e.memset(m[:, :], 0.0), [], "ident")
                alone(lambda e, i, m=m: e.affine_select(
                    out=m[:, :], in_=m[:, :], compare_op=ALU.not_equal, fill=1.0, base=0,
                    pattern=[[-1, P]], channel_multiplier=1), [], "ident")
            for m, sign, at_first, fill in ((mask, 1, 0.0, BIG), (mask_t, -1, 0.0, BIG), (seen, -1, 1.0, 0.0)):
                alone(lambda e, i, m=m, v=at_first: e.memset(m[:, :], v), [], "mask")
                for h in range(2):
                    alone(lambda e, i, m=m[BLK * h:BLK * h + BLK, :], sign=sign, fill=fill: e.affine_select(
                        out=m, in_=m, compare_op=ALU.is_ge, fill=fill, base=0, pattern=[[-sign, BLK]],
                        channel_multiplier=sign), [], "mask")
            for t in diag.values():
                put("dve", lambda e, i, t=t: e.memset(t[:, :, :, :].rearrange("p a b c -> p (a b c)").bitcast(F32), 0.0), done="zeroed")
            for t in stack.values():
                put("dve", lambda e, i, t=t: e.memset(t[:, :, :].rearrange("p a c -> p (a c)").bitcast(F32), 0.0), done="zeroed")
            for t in vals.values():
                alone(lambda e, i, t=t: e.memset(t[:, :, :, :], 0.0), [], "vals1")
                for h in range(2):
                    alone(lambda e, i, v=t[BLK * h:BLK * h + BLK, :, :, 16 * h + D:16 * h + D + 1]: e.memset(v, 1.0), [], "vals1")
            put("dve", lambda e, i: e.memset(ones_b[:, :], 1.0), done="ones")
            put("dve", lambda e, i: e.memset(rowmax[:, :], 0.0), done="ones")
            put("dve", lambda e, i: e.memset(minus_half[:, :], -0.5), done="ones")
            for t in xnT.values():
                put("dve", lambda e, i, t=t: e.memset(t[:, 0:1], 0.0), done="ones")
            for h in range(2):
                for blk in range(NB):
                    put("sp", lambda e, i, h=h, blk=blk: e.dma_start(
                        diag["ka"][BLK * h + ROWS:BLK * h + ROWS + 3, :, blk, BLK * h:BLK * h + BLK],
                        ones_b[:, :].rearrange("p (a c) -> p a c", c=BLK)),
                        wait=["ones", "zeroed"], done="ones rows", dma="ones")

            def product(dst, lhsT, rhs, wait, name, scale=1.0, transpose=False, dims_first=False):
                ps, read = bank()
                m, n = dst.shape[0], dst.shape[-1]
                if transpose:
                    k = lhsT.shape[0]
                    put("pe", lambda e, i: e.transpose(ps[0:m, 0:n], lhsT, ident[0:k, 0:k]),
                        wait=[read, "weights", "ident", *wait], done=name + " product")
                else:
                    put("pe", lambda e, i: e.matmul(ps[0:m, 0:n], lhsT, rhs, start=True, stop=True),
                        wait=[read, "weights", *wait], done=name + " product")
                to, of = dst, ps[0:m, 0:n]
                if dims_first:
                    to, of = to.rearrange("c (d h) -> c h d", d=D), of.rearrange("c (h d) -> c h d", d=D)
                put("act", lambda e, i: e.activation(to, of, ACT.Copy, scale=scale),
                    wait=[name + " product"], done=name)
                pg.marks[read] = pg.marks[name]

            product(T_uq[:, :], w_in["uq"][:, :], None, [], "T_uq", transpose=True)
            for t, n in ((T_o, "o"), (T_r, "r"), (T_k, "k"), (T_v, "v")):
                product(t[:, :], w_in[n][:, :], None, [], "T_" + n, transpose=True, scale=0.5 if n == "v" else 1.0)
            product(M_qT[:, :], T_uq[:, :], w_in["dq"][:, :], ["T_uq"], "M_qT")
            product(M_q[:, :], w_in["dq"][:, :], T_uq[:, :], ["T_uq"], "M_q", scale=float(D) ** -0.5, dims_first=True)
            product(k_effT[:, :], w_in["uk"][:, :], M_qT[:, :], ["M_qT"], "k_effT")
            product(v_eff[:, :], w_in["uv"][:, :], T_o[:, :], ["T_o"], "v_eff")
            product(M_k[:, :], w_in["dkv"][:, :], k_effT[:, :], ["k_effT"], "M_k", dims_first=True)
            product(M_v[:, :], w_in["dkv"][:, :], v_eff[:, :], ["v_eff"], "M_v")
            for lane in ("pe", "act", "dve", "pool", "sp"):
                put(lane, lambda e, i: e.nop(), wait=["weights", "M_v", "mask", "ident", "vals1", "zeroed", "ones", "ones rows"])

        def layernorm(n, src, ready):
            s, m, r, o = stats[n], mv[n], rstd[n], xn[n]
            for k in range(NT):
                put("dve", lambda e, i, k=k: e.bn_stats(s[:, k, :], src[:, k, :]), wait=[ready], done=f"stats{n}")
            put("dve", lambda e, i: e.tensor_copy(last_stats[:, :], s[:, NT - 1, :]), wait=[f"stats{n}"])
            for k in range(NT):
                put("dve", lambda e, i, k=k: e.bn_aggr(m[:, k, :], s[:, k, :]), done=f"mv{n}")
            put("dve", lambda e, i: e.tensor_scalar(m[:, :, 1], m[:, :, 1], EPS, None, ALU.add),
                wait=[f"mv{n}"], done=f"var{n}")
            alone(lambda e, i: e.tensor_tensor(r[:, :], m[:, :, 1], minus_half[:, 0:1].to_broadcast([P, NT]), ALU.pow),
                  [f"var{n}", f"xn{n}"], f"rstd{n}")
            for k in range(NT):
                put("dve", lambda e, i, k=k: e.tensor_scalar(o[:, k, :], src[:, k, :], m[:, k, 0:1], r[:, k:k + 1],
                                                             ALU.subtract, ALU.mult),
                    wait=[f"rstd{n}", f"xn{n} transposed"], done=f"xn{n}")
            yield
            ps, read = bank()
            for k in range(NT):
                put("pe", lambda e, i, k=k: e.transpose(ps[:, P * k:P * k + P], o[:, k, :], ident[:, :]),
                    wait=[read, f"xn{n}"], done=f"xn{n} transposed" if k == NT - 1 else None)
            put("act", lambda e, i: e.activation(xnT[n][:, 1:T + 1], ps[:, :], ACT.Copy),
                wait=[f"xn{n} transposed", f"xnT{n} read", f"xnT{n} diff read"], done=f"xnT{n}")
            pg.marks[read] = pg.marks[f"xnT{n}"]
            yield

        def split(n, ps, read, filled):
            p, r = parts[n], rest[n]
            put("act", lambda e, i: e.activation(p[:, 0, :], ps[:, :], ACT.Copy),
                wait=[filled, f"scratch {n} written"], done=f"{n} part0")
            put("dve", lambda e, i: e.tensor_tensor(r[:, :], ps[:, :], p[:, 0, :], ALU.subtract),
                wait=[f"{n} part0", filled, f"{n} part2"], done=f"{n} rest")
            pg.marks[read] = pg.marks[f"{n} rest"]
            put("dve", lambda e, i: e.tensor_copy(p[:, 1, :], r[:, :]),
                wait=[f"{n} rest", f"scratch {n} written"], done=f"{n} part1")
            alone(lambda e, i: e.tensor_tensor(p[:, 2, :], r[:, :], p[:, 1, :], ALU.subtract),
                [f"{n} rest", f"{n} part1", f"scratch {n} written"], f"{n} part2")
            side = 1 if n == "q" else 2
            for run in STACK:
                first, chosen = run[0], run[side]
                src = (p[:, chosen[0]:chosen[0] + 1, :].to_broadcast([P, len(chosen), T]) if chosen[0] == chosen[-1]
                       else p[:, 0:len(chosen), :])
                put("sp", lambda e, i, src=src, first=first, c=len(chosen): e.dma_start(
                    scratch[n][first:first + c].rearrange("t r c -> r t c"), src),
                    wait=[f"{n} part0", f"{n} part2", f"scratch {n} read"], done=f"scratch {n} written", dma="scr_" + n)

        def restack(n, to):
            for h in range(2):
                src = scratch[n].rearrange("t (d a h) c -> (t d) a h c", d=D, h=2)[:, :, h, :]
                put("sp", lambda e, i, src=src, h=h: e.dma_start(stack[to][BLK * h:BLK * h + ROWS, :, :], src),
                    wait=[f"scratch {n} written", f"stack {to} read", f"stack {to} copied"],
                    done=f"scratch {n} read", dma="stk_" + to)
            pg.marks[f"stack {to}"] = pg.marks[f"scratch {n} read"]

        def spread(n, frm):
            for h in range(2):
                rows = slice(BLK * h, BLK * h + ROWS)
                put("dve", lambda e, i, rows=rows, h=h: e.tensor_copy(
                    diag[n][rows, :, :, BLK * h:BLK * h + BLK],
                    stack[frm][rows, :, :].rearrange("p a (b c) -> p a b c", c=BLK)),
                    wait=[f"stack {frm}", f"diag {n} read"], done=f"diag {n}")
            pg.marks[f"stack {frm} copied"] = pg.marks[f"diag {n}"]

        def values(a, n, w):
            for half in range(2):
                ps, read = bank()
                for k in range(NB // 2):
                    c = 1 + BLK * (k + half * NB // 2)
                    keys = xnT[n][:, c:c + BLK]
                    for h in range(2):
                        put("pe", lambda e, i, k=k, h=h, keys=keys, ps=ps: e.matmul(
                            ps[BLK * h:BLK * h + BLK, P * k:P * k + P], keys, w, start=True, stop=True),
                            wait=[read, f"xnT{n}"], done=f"v{a}" if k == NB // 2 - 1 and h == 1 else None)
                pg.marks[f"xnT{n} read"] = pg.marks[f"v{a}"]
                for h in range(2):
                    r = slice(BLK * h, BLK * h + BLK)
                    put("act", lambda e, i, r=r, h=h, half=half, ps=ps: e.activation(
                        vals[a][r, NB // 2 * half:NB // 2 * (half + 1), :, 16 * h:16 * h + D],
                        ps[r, :].rearrange("p (b a h d) -> p b a h d", b=NB // 2, a=PAIRS, h=2)[:, :, :, h, :], ACT.Copy),
                        wait=[f"v{a}", f"vals {a} read"], done=f"vals {a}")
                pg.marks[read] = pg.marks[f"vals {a}"]
                yield

        tokens = [[C, P], [P * C, NT], [1, C]]

        def start_of(b):
            return lambda e, i: b * T * C if isinstance(i, int) else e.snap(i * (T * C) + b * T * C)

        def prepare(b):
            put("sp", lambda e, at: e.dma_start(xs["in"][:, :, :], bass.AP(x.tensor, at, tokens)), first=start_of(b),
                wait=["x_a"], done="x loaded", dma="x")
            yield
            yield from layernorm("1", xs["in"], "x loaded")
            for n, w in (("q", M_q), ("k", M_k)):
                ps, read = bank()
                put("pe", lambda e, i, w=w, ps=ps: e.matmul(
                    ps[:, :], w[:, :], xnT["1"][:, 1:T + 1], start=True, stop=True),
                    wait=[read, "xnT1"], done=f"{n} projected")
                split(n, ps, read, f"{n} projected")
                yield
                restack(n, "qa" if n == "q" else "k")
            yield from values("a", "1", M_v[:, :])
            spread("qa", "qa")
            yield
            for step in tiles_of_keys():
                for pair in range(PAIRS):
                    whole = len(step) == 1 and step[0][0] == 0
                    if step[0][0] == NB // 2 and pair % 2:
                        continue
                    ps, read = bank()
                    if whole:
                        todo = [(pair, NB - 1, 0)]
                    elif len(step) == 2:
                        i1 = NB - 1 - step[0][0]
                        todo = [(pair, i1, 0), (pair, step[0][0] - 1, BLK * (i1 + 1))]
                    else:
                        todo = [(pair, NB // 2 - 1, 0), (pair + 1, NB // 2 - 1, BANK // 2)]
                    for pr, q, at in todo:
                        put("pe", lambda e, i, pr=pr, q=q, at=at, ps=ps: e.matmul(
                            ps[:, at:at + BLK * (q + 1)], diag["qa"][:, pr, q, :], stack["k"][:, pr, 0:BLK * (q + 1)],
                            start=True, stop=False), wait=[read, "diag qa", "stack k"])
                        put("pe", lambda e, i, q=q, at=at, ps=ps: e.matmul(
                            ps[:, at + BLK * q:at + BLK * (q + 1)], ident_b[:, :], mask[:, :], start=False, stop=True),
                            done="raw scores")
                    for pr, q, at in todo:
                        put("dve", lambda e, i, pr=pr, q=q, at=at, ps=ps: e.tensor_reduce(
                            rowmax[:, pr * NB + q:pr * NB + q + 1], ps[:, at:at + BLK * (q + 1)], axis=AX.X, op=ALU.max),
                            wait=["raw scores", "rowmax read"], done="rowmax")
                    pg.marks[read] = pg.marks["rowmax"]
                    if pair % 2:
                        yield
            pg.marks["stack k read"] = pg.marks["diag qa read"] = pg.marks["raw scores"]
            yield
            ps, read = bank()
            n = PAIRS * NB
            put("pe", lambda e, i: e.transpose(ps[:, 0:P], rowmax[:, :], ident[:, :]), wait=[read, "rowmax"], done="rowmax read")
            put("act", lambda e, i: e.activation(mparts[:, 0, :], ps[0:n, 0:P], ACT.Copy, scale=-1.0),
                wait=["rowmax read", "max rows"], done="max part0")
            put("dve", lambda e, i: e.scalar_tensor_tensor(mrest[:, :], ps[0:n, 0:P], -1.0, mparts[:, 0, :], ALU.mult, ALU.subtract),
                wait=["max part0", "rowmax read"], done="max rest")
            pg.marks[read] = pg.marks["max rest"]
            put("dve", lambda e, i: e.tensor_copy(mparts[:, 1, :], mrest[:, :]), wait=["max rest", "max rows"], done="max part1")
            put("dve", lambda e, i: e.tensor_tensor(mparts[:, 2, :], mrest[:, :], mparts[:, 1, :], ALU.subtract),
                wait=["max part1"], done="max part2")
            for h in range(2):
                for part in range(3):
                    row = BLK * h + ROWS + part
                    put("sp", lambda e, i, h=h, part=part, row=row: e.dma_start(
                        stack["qa"][row:row + 1, :, :], mparts[:, part, BLK * h:BLK * h + BLK]),
                        wait=["max part0", "max part2", "stack qa read", "stack qa copied"], done="max rows", dma="max")
            spread("ka", "k")
            yield

        unit = [0]

        def attend(a, scale):
            q, kd = stack["q" + a], diag["k" + a]
            ready = [f"stack q{a}", f"diag k{a}"] + (["max rows"] if a == "a" else [])
            for g in range(GROUPS):
                waiting = None
                for s, step in enumerate([*tiles_of_keys(), None]):
                    placed = []
                    if step is not None:
                        half = step[0][0] == NB // 2
                        for u in range(1 if half else 2):
                            n, t = unit[0], unit[0] % 2
                            unit[0] += 1
                            for k in range(2):
                                todo = ([(2 * k + z, NB // 2, z * BANK // 2) for z in range(2)] if half
                                        else [(2 * u + k, blk, at) for blk, at in step])
                                for j, blk, at in todo:
                                    pair, width = GROUP * g + j, T - BLK * blk
                                    put("pe", lambda e, i, t=t, k=k, at=at, width=width, pair=pair, blk=blk: e.matmul(
                                        score[t][:, k, at:at + width], kd[:, pair, blk, :], q[:, pair, BLK * blk:T],
                                        start=True, stop=a == "b"),
                                        wait=[f"score{t} read", *ready], done=f"scores{t}")
                                    if a == "a":
                                        put("pe", lambda e, i, t=t, k=k, at=at: e.matmul(
                                            score[t][:, k, at:at + BLK], ident_b[:, :], mask_t[:, :], start=False, stop=True),
                                            done=f"scores{t}")
                                    placed.append((j, blk, n % NPROB, k, at))
                            pr = prob[n % NPROB]
                            put("act", lambda e, i, t=t, pr=pr: e.activation(
                                pr[:, :, :], score[t][:, :, :], ACT.Exp, scale=scale),
                                wait=[f"scores{t}", f"prob{n % NPROB} read"], done=f"score{t} read")
                            if a == "a":
                                pg.marks[f"prob{n % NPROB}"] = pg.marks[f"score{t} read"]
                                continue
                            blocks = 1 if step[0][0] == 0 else 2
                            gap = BANK // 2 if half else T - BLK * step[0][0]
                            start = bass.AP(pr, 0, [[2 * BANK, P], [BANK, 2], [gap, blocks], [1, BLK]])
                            alone(lambda e, i, start=start, blocks=blocks: e.tensor_tensor(
                                start, start, seen[:, :].rearrange("p (a b c) -> p a b c", a=1, b=1).to_broadcast([P, 2, blocks, BLK]),
                                ALU.mult), [f"score{t} read"], f"prob{n % NPROB}")
                    if waiting:
                        last = s == len(tiles_of_keys())
                        for blk in sorted({w[1] for w in waiting}):
                            for j, b_, slot, k, at in [w for w in waiting if w[1] == blk]:
                                width = T - BLK * blk
                                put("pe", lambda e, i, g=g, j=j, blk=blk, slot=slot, k=k, at=at, width=width: e.matmul(
                                    acc[32 * j:32 * j + 32, BLK * blk:T], vals[a][:, blk, GROUP * g + j, :],
                                    prob[slot][:, k, at:at + width], start=blk == 0, stop=blk == NB // 2),
                                    wait=[f"prob{slot}", "acc read", f"vals {a}"], done=f"prob{slot} read")
                                pg.marks[f"{a} summed"] = pg.marks[f"prob{slot} read"]
                    waiting = placed
                    yield
                put("act", lambda e, i, g=g: e.activation(outT[a][g][:, :], acc[:, :], ACT.Copy),
                    wait=[f"{a} summed", f"outT{a}{g} read"], done="acc read")
                pg.marks[f"outT{a}{g}"] = pg.marks["acc read"]
            pg.marks[f"vals {a} read"] = pg.marks[f"stack q{a} read"] = pg.marks[f"diag k{a} read"] = pg.marks[f"{a} summed"]

        def normalise(a):
            for g in range(GROUPS):
                ps, read = bank()
                src = outT[a][g]
                for k in range(NT):
                    put("pe", lambda e, i, k=k, ps=ps, src=src: e.transpose(
                        ps[:, P * k:P * k + P], src[:, P * k:P * k + P], ident[:, :]),
                        wait=[read, f"outT{a}{g}"], done=f"outT{a}{g} read" if k == NT - 1 else None)
                heads = ps[:, :].rearrange("p (k h c) -> p k h c", k=NT, c=16)
                put("dve", lambda e, i, heads=heads, g=g: e.reciprocal(
                    rden[a][g][:, :].rearrange("p (k h) -> p k h", k=NT), heads[:, :, :, D]),
                    wait=[f"outT{a}{g} read"], done=f"rden{a}{g}")
                w = 2 * GROUP * D
                put("dve", lambda e, i, heads=heads, g=g, w=w: e.tensor_tensor(
                    y[a][:, :, w * g:w * g + w].rearrange("p k (h d) -> p k h d", d=D), heads[:, :, :, 0:D],
                    rden[a][g][:, :].rearrange("p (k h o) -> p k h o", k=NT, o=1).to_broadcast([P, NT, 2 * GROUP, D]),
                    ALU.mult), wait=[f"rden{a}{g}", f"y{a} read"], done=f"y{a}")
                pg.marks[read] = pg.marks[f"y{a}"]
                yield

        def after_a():
            yield from normalise("a")
            alone(lambda e, i: e.tensor_tensor(xs["a"][:, :, :], xs["in"][:, :, :], y["a"][:, :, :], ALU.add),
                ["ya", "x_ffn"], "x_a")
            pg.marks["ya read"] = pg.marks["x_a"]
            yield

        def feed_forward(n, src, dst, dst_free, result):
            f = ffn[n]
            now, before = xnT[n][:, 1:T + 1], xnT[n][:, 0:T]
            alone(lambda e, i: e.tensor_tensor(f["diff"][:, :], now, before, ALU.subtract),
                [f"xnT{n}", f"mixed{n}"], f"xnT{n} diff read")
            for k, b in enumerate(("xk", "xr")):
                put("dve", lambda e, i, k=k, b=b: e.scalar_tensor_tensor(
                    f[b][:, :], f["diff"][:, :], mu[:, 1 - k:2 - k], before, ALU.mult, ALU.add),
                    wait=[f"xnT{n} diff read", f"ffn{n} {b} read"], done=f"ffn{n} {b}")
            pg.marks[f"mixed{n}"] = pg.marks[f"xnT{n} read"] = pg.marks[f"ffn{n} xr"]
            yield
            ps, read = bank()
            put("pe", lambda e, i, ps=ps: e.matmul(ps[:, :], T_k[:, :], f["xk"][:, :], start=True, stop=True),
                wait=[read, f"ffn{n} xk"], done=f"ffn{n} xk read")
            put("act", lambda e, i, ps=ps: e.activation(f["act"][:, :], ps[:, :], ACT.Relu),
                wait=[f"ffn{n} xk read", f"ffn{n} act read"], done=f"ffn{n} relu")
            pg.marks[read] = pg.marks[f"ffn{n} relu"]
            alone(lambda e, i: e.tensor_tensor(f["act"][:, :], f["act"][:, :], f["act"][:, :], ALU.mult),
                [f"ffn{n} relu", f"ffn{n} act read"], f"ffn{n} act")
            ps, read = bank()
            for k in range(NT):
                put("pe", lambda e, i, k=k, ps=ps: e.matmul(ps[:, P * k:P * k + P], f["xr"][:, P * k:P * k + P], T_r[:, :],
                                                            start=True, stop=True),
                    wait=[read, f"ffn{n} xr"], done=f"ffn{n} xr read" if k == NT - 1 else None)
            put("act", lambda e, i, ps=ps: e.activation(f["gate"][:, :], ps[:, :], ACT.Tanh, scale=0.5),
                wait=[f"ffn{n} xr read", f"ffn{n} prod"], done=f"ffn{n} gate")
            pg.marks[read] = pg.marks[f"ffn{n} gate"]
            yield
            ps, read = bank()
            for k in range(NT):
                put("pe", lambda e, i, k=k, ps=ps: e.matmul(ps[:, P * k:P * k + P], f["act"][:, P * k:P * k + P], T_v[:, :],
                                                            start=True, stop=True),
                    wait=[read, f"ffn{n} act"], done=f"ffn{n} act read" if k == NT - 1 else None)
            put("dve", lambda e, i, ps=ps: e.scalar_tensor_tensor(f["diff"][:, :], f["gate"][:, :], 1.0, ps[:, :],
                                                                  ALU.add, ALU.mult),
                wait=[f"ffn{n} act read", f"ffn{n} gate", result], done=f"ffn{n} prod")
            pg.marks[read] = pg.marks[f"ffn{n} prod"]
            alone(lambda e, i: e.tensor_tensor(dst[:, :, :], src[:, :, :],
                                                     f["diff"][:, :].rearrange("p (k c) -> p k c", k=NT), ALU.add),
                wait=[f"ffn{n} prod", dst_free], done=result)
            yield

        def middle():
            yield from layernorm("2", xs["a"], "x_a")
            yield from feed_forward("2", xs["a"], xs["ffn"], "x_b", "x_ffn")
            yield from layernorm("3", xs["ffn"], "x_ffn")
            for half in range(2):
                ps, read = bank()
                for k in range(2):
                    tile = 2 * half + k
                    put("pe", lambda e, i, k=k, tile=tile, ps=ps: e.matmul(
                        ps[:, 2 * C * k:2 * C * (k + 1)], xnT["3"][:, 1 + P * tile:1 + P * (tile + 1)],
                        w_qk[:, :, :].rearrange("p a c -> p (a c)"), start=True, stop=True),
                        wait=[read, "xnT3"], done="qk projected" if k else None)
                two = slice(2 * half, 2 * half + 2)
                put("act", lambda e, i, two=two, ps=ps: e.activation(
                    qk[:, two, :, :].rearrange("p k a c -> p k (a c)"), ps[:, :].rearrange("p (k c) -> p k c", k=2), ACT.Square),
                ["qk projected", "qk read"], "squares")
                put("dve", lambda e, i, two=two: e.tensor_reduce(
                    ssum[:, two, :], qk[:, two, :, :].rearrange("p k a (h d) -> p k (a h) d", d=D), axis=AX.X, op=ALU.add),
                    wait=["squares", "rnorm"], done="norms2")
                put("dve", lambda e, i, two=two: e.tensor_scalar(ssum[:, two, :], ssum[:, two, :], 1e-24, None, ALU.max),
                    wait=["norms2"], done="norms2 kept up")
                alone(lambda e, i, two=two: e.tensor_tensor(
                    rnorm[:, two, :], ssum[:, two, :],
                    minus_half[:, :].rearrange("p (a b) -> p a b", a=1).to_broadcast([P, 2, 2 * HEADS]), ALU.pow),
                      ["norms2 kept up", "qk"], "rnorm")
                for k in range(2):
                    tile = 2 * half + k
                    put("dve", lambda e, i, k=k, tile=tile, ps=ps: e.tensor_tensor(
                        qk[:, tile, :, :].rearrange("p a (d h) -> p a h d", d=D),
                        ps[:, 2 * C * k:2 * C * (k + 1)].rearrange("p (a h d) -> p a h d", a=2, d=D),
                        rnorm[:, tile, :].rearrange("p (a h o) -> p a h o", a=2, o=1).to_broadcast([P, 2, HEADS, D]), ALU.mult),
                        wait=["rnorm", "qk projected", "qk read"], done="qk")
                pg.marks[read] = pg.marks["qk"]
                yield
            pg.marks["xnT3 read"] = pg.marks["qk projected"]
            yield from values("b", "3", w_v[:, :])
            for a, n in enumerate("qk"):
                ps, read = bank()
                for k in range(NT):
                    put("pe", lambda e, i, k=k, a=a, ps=ps: e.transpose(ps[:, P * k:P * k + P], qk[:, k, a, :], ident[:, :]),
                        wait=[read, "qk"], done=f"{n} turned" if k == NT - 1 else None)
                split(n, ps, read, f"{n} turned")
                yield
                restack(n, "qb" if n == "q" else "k")
            pg.marks["qk read"] = pg.marks["k turned"]
            yield
            spread("kb", "k")
            yield

        def finish(b):
            yield from normalise("b")
            ps, read = bank()
            for k in range(NT):
                put("pe", lambda e, i, k=k, ps=ps: e.transpose(ps[:, P * k:P * k + P], y["b"][:, k, :], ident[:, :]),
                    wait=[read, "yb"], done="yb read" if k == NT - 1 else None)
            put("act", lambda e, i, ps=ps: e.activation(yT[:, :], ps[:, :], ACT.Copy), wait=["yb read", "yT read"], done="yT")
            pg.marks[read] = pg.marks["yT"]
            yield
            ps, read = bank()
            for k in range(NT):
                put("pe", lambda e, i, k=k, ps=ps: e.matmul(ps[:, P * k:P * k + P], yT[:, P * k:P * k + P], w_ob[:, :],
                                                            start=True, stop=True),
                    wait=[read, "yT"], done="yT read" if k == NT - 1 else None)
            put("dve", lambda e, i, ps=ps: e.tensor_tensor(xs["b"][:, :, :], ps[:, :].rearrange("p (k c) -> p k c", k=NT),
                                                           xs["ffn"][:, :, :], ALU.add),
                wait=["yT read", "x_ffn", "x_out"], done="x_b")
            pg.marks[read] = pg.marks["x_b"]
            yield
            yield from layernorm("4", xs["b"], "x_b")
            yield from feed_forward("4", xs["b"], xs["out"], "stored", "x_out")
            put("sp", lambda e, at: e.dma_start(bass.AP(out.tensor, at, tokens), xs["out"][:, :, :]), first=start_of(b),
                wait=["x_out"], done="stored", dma="out")
            yield

        def weave(main, side, n_main, n_side):
            done = 0
            for m in range(n_main):
                if main:
                    next(main, None)
                while side and done * n_main < (m + 1) * n_side:
                    next(side, None)
                    done += 1
            for gen in (main, side):
                for _ in gen or ():
                    pass

        def turns(*gens):
            gens = [g for g in gens if g]
            while gens:
                for g in list(gens):
                    try:
                        next(g)
                        yield
                    except StopIteration:
                        gens.remove(g)

        def iteration(t):
            live = lambda b: 0 <= b < B
            side = turns(finish(t - 2) if live(t - 2) else None, middle() if live(t - 1) else None)
            weave(attend("a", 1.0) if live(t) else None, side, 12, 28)
            if live(t):
                for _ in after_a():
                    pass
            weave(attend("b", 8.0) if live(t - 1) else None, prepare(t + 1) if live(t + 1) else None, 12, 32)

        pieces = []
        setup()
        weave(None, prepare(0), 0, 0)
        for t in range(3):
            iteration(t)
        pieces.append((pg.cut(), 1, None))
        first, last = 3, B - 2
        assert last > first

        def shape(items, counts):
            return [[(s.sem.name, v - counts[s]) for s, v in waits] for waits, *_ in items]

        kept = None
        for t in range(first, last + 1):
            before, r0, u0 = pg.counts(), ring[0], unit[0]
            iteration(t)
            piece = pg.cut()
            assert (ring[0] - r0) % 3 == 0 and (unit[0] - u0) % 2 == 0 and (unit[0] - u0) % NPROB == 0, (ring[0] - r0, unit[0] - u0)
            grow = {s: n - before[s] for s, n in pg.counts().items()}
            form = {k: shape(v, before) for k, v in piece.items()}
            if kept is None:
                kept = (piece, grow, form)
            assert kept[1] == grow and kept[2] == form, "turns of the loop differ"
        pieces.append((kept[0], last - first + 1, kept[1]))
        for t in range(last + 1, B + 2):
            iteration(t)
        put("sp", lambda e, i: e.nop(), wait=["stored"])
        pieces.append((pg.cut(), 1, None))

        block = ctx.enter_context(nc.Block())

        def run(name, eng):
            for items, count, grow in pieces:
                if count == 1:
                    emit(eng, items[name])
                else:
                    with eng.Fori(0, count) as i:
                        emit(eng, items[name], i, grow)

        @block.sync
        def _(eng):
            run("sp", eng)

        @block.gpsimd
        def _(eng):
            run("pool", eng)

        @block.scalar
        def _(eng):
            run("act", eng)

        @block.vector
        def _(eng):
            run("dve", eng)

        @block.tensor
        def _(eng):
            run("pe", eng)


_NAMES = ["L0_attn_a_x", "L0_attn_a_W_dq", "L0_attn_a_W_uq", "L0_attn_a_W_dkv", "L0_attn_a_W_uk", "L0_attn_a_W_uv",
          "L0_attn_a_W_o", "L0_attn_b_Wq", "L0_attn_b_Wk", "L0_attn_b_Wv", "L0_attn_b_Wo",
          "L0_ffn_W_r", "L0_ffn_W_k", "L0_ffn_W_v", "L0_ffn_mu_r", "L0_ffn_mu_k"]


def kernel(**inputs):
    import concourse.bacc as bacc
    from concourse.bass_utils import run_bass_kernel_spmd

    nc = bacc.Bacc("TRN2", target_bir_lowering=False, num_devices=1)
    arrays, args = {}, []
    for name in _NAMES:
        a = np.ascontiguousarray(inputs[name])
        arrays["in_" + name] = a
        args.append(nc.dram_tensor("in_" + name, a.shape, mybir.dt.from_np(a.dtype), kind="ExternalInput").ap())
    shape = inputs["L0_attn_a_x"].shape
    args.append(nc.dram_tensor("out_0", shape, F32, kind="ExternalOutput").ap())
    build(nc, *args)
    r = run_bass_kernel_spmd(nc, [arrays], core_ids=[0])
    return r.results[0]["out_0"]
```

```python
import numpy as np
import concourse.bass as bass
from concourse import mybir
from contextlib import ExitStack

F32, BF16 = mybir.dt.float32, mybir.dt.bfloat16
ALU, ACT, AX = mybir.AluOpType, mybir.ActivationFunctionType, mybir.AxisListType

P = 128
HEADS = 16
PAIRS = HEADS // 2
GROUP = 4
GROUPS = PAIRS // GROUP
BLK = 64
BANK = 512
ROWS = 48
BIG = -3.0e38
EPS = 1e-5
STACK = [(0, (0, 0, 0), (0, 1, 2)), (3, (1, 1), (0, 1)), (5, (2,), (0,))]
PRODUCTS = 6


class Lane:

    def __init__(self, sem, by=1):
        self.sem, self.by, self.count, self.items, self.seen = sem, by, 0, [], {}

    def mark(self):
        self.count += self.by
        return (self, self.count)


class Program:

    def __init__(self, engines, dmas):
        self.lanes, self.dmas, self.marks = engines, dmas, {}

    def put(self, lane, make, wait=(), done=None, dma=None, first=None):
        line, waits = self.lanes[lane], []
        for name in wait:
            m = self.marks.get(name)
            if m and line.seen.get(m[0], 0) < m[1]:
                line.seen[m[0]] = m[1]
                waits.append(m)
        inc = None
        if done is not None:
            source = self.dmas[dma] if dma else line
            self.marks[done] = source.mark()
            inc = (source.sem, source.by)
        line.items.append((waits, make, inc, first))

    def cut(self):
        piece = {k: v.items for k, v in self.lanes.items()}
        for v in self.lanes.values():
            v.items, v.seen = [], {}
        return piece

    def counts(self):
        return {x: x.count for x in [*self.lanes.values(), *self.dmas.values()]}


def emit(engine, items, i=0, grow=None):
    for waits, make, inc, first in items:
        arg = first(engine, i) if first else i
        values = [i * grow[source] + value if grow else value for source, value in waits]
        for value in values if grow else ():
            engine.compute_val(value)
        for (source, _), value in zip(waits, values):
            engine.wait_ge(source.sem, value)
        made = make(engine, arg)
        if inc:
            made.then_inc(*inc)


def tiles_of_keys():
    n = BANK // BLK
    return [[(0, 0)]] + [[(i, 0), (n - i, BANK - BLK * i)] for i in range(1, n // 2)] + [[(n // 2, 0)]]


def build(nc, x, wdq, wuq, wdkv, wuk, wuv, wo_a, wq, wk, wv, wo_b, wr, wkf, wvf, mur, muk, out):
    B, T, C = x.shape
    NT = T // P
    NB = T // BLK
    D = C // HEADS
    QL, KVL = wdq.shape[0], wdkv.shape[0]
    W = {'ahead': 6, 'b0': 3, 'max': [0, 12], 'rows': [13, 14], 'mb': [0, 24], 'fin': [0, 34], 'pf': [12, 34], 'keep': [22, 23], 'kb': [30, 35], 'na': [24, 25], 'mf': [0, 25], 'pb': [0, 35]}
    NPROB = 4

    ctx = ExitStack()
    with ctx:
        def sb(name, shape, dt=F32):
            return ctx.enter_context(nc.sbuf_tensor(name, shape, dt))

        def sem(name):
            return ctx.enter_context(nc.semaphore(name))

        ident = sb("ident", [P, P])
        ident_b = sb("ident_b", [P, P], BF16)
        ones_b = sb("ones_b", [3, PAIRS * BLK], BF16)
        last_stats = sb("last_stats", [P, 6])
        mask = sb("mask", [P, BLK], BF16)
        mask_t = sb("mask_t", [P, BLK], BF16)
        seen = sb("seen", [P, BLK])
        minus_half = sb("minus_half", [P, 1])
        w_in = {n: sb("raw_" + n, list(a.shape)) for n, a in
                dict(dq=wdq, uq=wuq, dkv=wdkv, uk=wuk, uv=wuv, o=wo_a, r=wr, k=wkf, v=wvf).items()}
        w_qk = sb("w_qk", [P, 2, C])
        w_v = sb("w_v", [P, C])
        w_ob = sb("w_ob", [P, C])
        mu = sb("mu", [P, 2])
        T_uq = sb("T_uq", [QL, C])
        T_o = sb("T_o", [P, C])
        T_r = sb("T_r", [P, C])
        T_k = sb("T_k", [P, C])
        T_v = sb("T_v", [P, C])
        M_q = sb("M_q", [P, C])
        M_qT = sb("M_qT", [P, C])
        k_effT = sb("k_effT", [KVL, C])
        v_eff = sb("v_eff", [KVL, C])
        M_k = sb("M_k", [P, C])
        M_v = sb("M_v", [P, C])
        xs = {n: sb("x_" + n, [P, NT, C]) for n in ("in", "again", "a", "ffn", "kept", "b", "out")}
        stats = {n: sb(f"stats_{n}", [P, NT, 6]) for n in ("1", "2", "3", "4")}
        mv = {n: sb(f"mv_{n}", [P, NT, 2]) for n in stats}
        rstd = {n: sb(f"rstd_{n}", [P, NT]) for n in stats}
        xn = {n: sb(f"xn_{n}", [P, NT, C]) for n in stats}
        xnT = {n: sb(f"xnT_{n}", [P, T + 1]) for n in stats}
        ffn = {n: sb("ffn_" + n, [P, T]) for n in ("diff", "xr", "xk", "act", "gate", "prod")}
        parts = {n: sb("parts_" + n, [P, 3, T], BF16) for n in "qk"}
        rest = {n: sb("rest_" + n, [P, T]) for n in parts}
        stack = {n: sb("stack_" + n, [P, PAIRS, T], BF16) for n in ("qa", "qb", "k")}
        diag = {n: sb("diag_" + n, [P, PAIRS, NB, P], BF16) for n in ("qa", "ka", "kb")}
        vals = {n: sb("vals_" + n, [P, NB, PAIRS, 32]) for n in "ab"}
        rowmax = [sb(f"rowmax{g}", [P, P]) for g in range(GROUPS)]
        mparts = [sb(f"mparts{g}", [GROUP * NB, 3, P], BF16) for g in range(GROUPS)]
        mrest = [sb(f"mrest{g}", [GROUP * NB, P]) for g in range(GROUPS)]
        prob = [sb(f"prob{i}", [P, 2, BANK]) for i in range(NPROB)]
        outT = {n: [sb(f"outT_{n}{g}", [P, T]) for g in range(GROUPS)] for n in "ab"}
        rden = {n: [sb(f"rden_{n}{g}", [P, NT * 2 * GROUP]) for g in range(GROUPS)] for n in "ab"}
        y = {n: sb("y_" + n, [P, NT, C]) for n in "ab"}
        yT = sb("yT", [P, T])
        raw = sb("raw", [P, NT, 2, C])
        qk = sb("qk", [P, NT, 2, C])
        ssum = sb("ssum", [P, NT * 2 * HEADS])
        rnorm = sb("rnorm", [P, NT * 2 * HEADS])
        step_r = sb("step_r", [P, NT * 2 * HEADS])

        def pb(name, shape, dt=F32):
            return ctx.enter_context(nc.psum_tensor(name, shape, dt))

        score = [pb(f"score{i}", [P, 2, BANK]) for i in range(2)]
        acc = pb("acc", [P, BANK])
        misc = [pb(f"misc{i}", [P, BANK]) for i in range(3)]

        scratch = {n: nc.dram_tensor("scratch_" + n, (PRODUCTS, P, T), BF16, kind="Internal").ap()
                   for n in ("qa", "ka", "qb", "kb")}

        lanes = {n: Lane(sem("s_" + n)) for n in ("pe", "act", "dve", "pool", "sp")}
        dmas = {n: Lane(sem("s_dma_" + n), 16) for n in
                ["w", "x", "again", "keep", "out", "max0", "max1", "ones"] + ["out_" + n for n in scratch] + ["in_" + n for n in scratch]}
        pg = Program(lanes, dmas)
        put = pg.put

        def alone(make, wait, done):
            put("pool", make, wait=["pool before", *wait], done=done)
            pg.marks["pool before"] = pg.marks[done]

        ring, unit = [0], [0]

        def bank():
            k = ring[0] % 3
            ring[0] += 1
            return misc[k], f"misc{k} read"

        def setup():
            loads = [(w_in["dq"], wdq), (w_in["uq"], wuq), (w_in["dkv"], wdkv), (w_in["uk"], wuk),
                     (w_in["uv"], wuv), (w_in["o"], wo_a), (w_in["r"], wr), (w_in["k"], wkf), (w_in["v"], wvf)]
            for dst, src in loads:
                put("sp", lambda e, i, d=dst, s=src: e.dma_start(d[:, :], s), done="weights", dma="w")
            for dst, src in [(w_qk[:, 0, :], wq), (w_qk[:, 1, :], wk), (w_v[:, :], wv), (w_ob[:, :], wo_b),
                             (mu[:, 0:1], mur.rearrange("(c o) -> c o", o=1)),
                             (mu[:, 1:2], muk.rearrange("(c o) -> c o", o=1))]:
                put("sp", lambda e, i, d=dst, s=src: e.dma_start(d, s), done="weights", dma="w")
            for m in (ident, ident_b):
                alone(lambda e, i, m=m: e.memset(m[:, :], 0.0), [], "ident")
                alone(lambda e, i, m=m: e.affine_select(
                    out=m[:, :], in_=m[:, :], compare_op=ALU.not_equal, fill=1.0, base=0,
                    pattern=[[-1, P]], channel_multiplier=1), [], "ident")
            for m, sign, at_first, fill in ((mask, 1, 0.0, BIG), (mask_t, -1, 0.0, BIG), (seen, -1, 1.0, 0.0)):
                alone(lambda e, i, m=m, v=at_first: e.memset(m[:, :], v), [], "mask")
                for h in range(2):
                    alone(lambda e, i, m=m[BLK * h:BLK * h + BLK, :], sign=sign, fill=fill: e.affine_select(
                        out=m, in_=m, compare_op=ALU.is_ge, fill=fill, base=0, pattern=[[-sign, BLK]],
                        channel_multiplier=sign), [], "mask")
            for t in diag.values():
                put("dve", lambda e, i, t=t: e.memset(t[:, :, :, :].rearrange("p a b c -> p (a b c)").bitcast(F32), 0.0), done="zeroed")
            for t in stack.values():
                put("dve", lambda e, i, t=t: e.memset(t[:, :, :].rearrange("p a c -> p (a c)").bitcast(F32), 0.0), done="zeroed")
            for t in vals.values():
                alone(lambda e, i, t=t: e.memset(t[:, :, :, :], 0.0), [], "vals1")
                for h in range(2):
                    alone(lambda e, i, v=t[BLK * h:BLK * h + BLK, :, :, 16 * h + D:16 * h + D + 1]: e.memset(v, 1.0), [], "vals1")
            put("dve", lambda e, i: e.memset(ones_b[:, :], 1.0), done="ones")
            for t in rowmax:
                put("dve", lambda e, i, t=t: e.memset(t[:, :], 0.0), done="ones")
            put("dve", lambda e, i: e.memset(minus_half[:, :], -0.5), done="ones")
            for t in xnT.values():
                put("dve", lambda e, i, t=t: e.memset(t[:, 0:1], 0.0), done="ones")
            for h in range(2):
                for blk in range(NB):
                    put("sp", lambda e, i, h=h, blk=blk: e.dma_start(
                        diag["ka"][BLK * h + ROWS:BLK * h + ROWS + 3, :, blk, BLK * h:BLK * h + BLK],
                        ones_b[:, :].rearrange("p (a c) -> p a c", c=BLK)),
                        wait=["ones", "zeroed"], done="ones rows", dma="ones")

            def product(dst, lhsT, rhs, wait, name, scale=1.0, transpose=False, dims_first=False):
                ps, read = bank()
                m, n = dst.shape[0], dst.shape[-1]
                if transpose:
                    k = lhsT.shape[0]
                    put("pe", lambda e, i: e.transpose(ps[0:m, 0:n], lhsT, ident[0:k, 0:k]),
                        wait=[read, "weights", "ident", *wait], done=name + " product")
                else:
                    put("pe", lambda e, i: e.matmul(ps[0:m, 0:n], lhsT, rhs, start=True, stop=True),
                        wait=[read, "weights", *wait], done=name + " product")
                to, of = dst, ps[0:m, 0:n]
                if dims_first:
                    to, of = to.rearrange("c (d h) -> c h d", d=D), of.rearrange("c (h d) -> c h d", d=D)
                put("act", lambda e, i: e.activation(to, of, ACT.Copy, scale=scale),
                    wait=[name + " product"], done=name)
                pg.marks[read] = pg.marks[name]

            product(T_uq[:, :], w_in["uq"][:, :], None, [], "T_uq", transpose=True)
            for t, n in ((T_o, "o"), (T_r, "r"), (T_k, "k"), (T_v, "v")):
                product(t[:, :], w_in[n][:, :], None, [], "T_" + n, transpose=True, scale=0.5 if n == "v" else 1.0)
            product(M_qT[:, :], T_uq[:, :], w_in["dq"][:, :], ["T_uq"], "M_qT")
            product(M_q[:, :], w_in["dq"][:, :], T_uq[:, :], ["T_uq"], "M_q", scale=float(D) ** -0.5, dims_first=True)
            product(k_effT[:, :], w_in["uk"][:, :], M_qT[:, :], ["M_qT"], "k_effT")
            product(v_eff[:, :], w_in["uv"][:, :], T_o[:, :], ["T_o"], "v_eff")
            product(M_k[:, :], w_in["dkv"][:, :], k_effT[:, :], ["k_effT"], "M_k", dims_first=True)
            product(M_v[:, :], w_in["dkv"][:, :], v_eff[:, :], ["v_eff"], "M_v")
            for lane in ("pe", "act", "dve", "pool", "sp"):
                put(lane, lambda e, i: e.nop(), wait=["weights", "M_v", "mask", "ident", "vals1", "zeroed", "ones", "ones rows"])

        def layernorm(n, src, ready):
            s, m, r, o = stats[n], mv[n], rstd[n], xn[n]
            for k in range(NT):
                put("dve", lambda e, i, k=k: e.bn_stats(s[:, k, :], src[:, k, :]), wait=[ready], done=f"stats{n}")
            put("dve", lambda e, i: e.tensor_copy(last_stats[:, :], s[:, NT - 1, :]), wait=[f"stats{n}"])
            for k in range(NT):
                put("dve", lambda e, i, k=k: e.bn_aggr(m[:, k, :], s[:, k, :]), done=f"mv{n}")
            put("dve", lambda e, i: e.tensor_scalar(m[:, :, 1], m[:, :, 1], EPS, None, ALU.add),
                wait=[f"mv{n}"], done=f"var{n}")
            alone(lambda e, i: e.tensor_tensor(r[:, :], m[:, :, 1], minus_half[:, 0:1].to_broadcast([P, NT]), ALU.pow),
                  [f"var{n}", f"xn{n}"], f"rstd{n}")
            yield
            yield
            for k in range(NT):
                put("dve", lambda e, i, k=k: e.tensor_scalar(o[:, k, :], src[:, k, :], m[:, k, 0:1], r[:, k:k + 1],
                                                             ALU.subtract, ALU.mult),
                    wait=[f"rstd{n}", f"xn{n} transposed"], done=f"xn{n}")
            yield
            ps, read = bank()
            for k in range(NT):
                put("pe", lambda e, i, k=k: e.transpose(ps[:, P * k:P * k + P], o[:, k, :], ident[:, :]),
                    wait=[read, f"xn{n}"], done=f"xn{n} transposed" if k == NT - 1 else None)
            put("act", lambda e, i: e.activation(xnT[n][:, 1:T + 1], ps[:, :], ACT.Copy),
                wait=[f"xn{n} transposed", f"xnT{n} read", f"xnT{n} diff read"], done=f"xnT{n}")
            pg.marks[read] = pg.marks[f"xnT{n}"]
            yield

        def split(n, a, ps, read, filled):
            p, r = parts[n], rest[n]
            put("act", lambda e, i: e.activation(p[:, 0, :], ps[:, :], ACT.Copy),
                wait=[filled, f"parts {n} written out"], done=f"{n} part0")
            put("dve", lambda e, i: e.tensor_tensor(r[:, :], ps[:, :], p[:, 0, :], ALU.subtract),
                wait=[f"{n} part0", filled, f"{n} part2"], done=f"{n} rest")
            pg.marks[read] = pg.marks[f"{n} rest"]
            put("dve", lambda e, i: e.tensor_copy(p[:, 1, :], r[:, :]),
                wait=[f"{n} rest", f"parts {n} written out"], done=f"{n} part1")
            alone(lambda e, i: e.tensor_tensor(p[:, 2, :], r[:, :], p[:, 1, :], ALU.subtract),
                [f"{n} rest", f"{n} part1", f"parts {n} written out"], f"{n} part2")
            side = 1 if n == "q" else 2
            for run in STACK:
                first, chosen = run[0], run[side]
                src = (p[:, chosen[0]:chosen[0] + 1, :].to_broadcast([P, len(chosen), T]) if chosen[0] == chosen[-1]
                       else p[:, 0:len(chosen), :])
                put("sp", lambda e, i, src=src, first=first, c=len(chosen): e.dma_start(
                    scratch[n + a][first:first + c].rearrange("t r c -> r t c"), src),
                    wait=[f"{n} part0", f"{n} part2", f"scratch {n}{a} read"], done=f"scratch {n}{a}", dma=f"out_{n}{a}")
            pg.marks[f"parts {n} written out"] = pg.marks[f"scratch {n}{a}"]

        def restack(n, a, to):
            for h in range(2):
                src = scratch[n + a].rearrange("t (d a h) c -> (t d) a h c", d=D, h=2)[:, :, h, :]
                put("sp", lambda e, i, src=src, h=h: e.dma_start(stack[to][BLK * h:BLK * h + ROWS, :, :], src),
                    wait=[f"scratch {n}{a}", f"stack {to} read", f"stack {to} copied"],
                    done=f"scratch {n}{a} read", dma=f"in_{n}{a}")
            pg.marks[f"stack {to}"] = pg.marks[f"scratch {n}{a} read"]

        def spread(n, frm):
            for g in range(GROUPS):
                pairs = slice(GROUP * g, GROUP * g + GROUP)
                for h in range(2):
                    rows = slice(BLK * h, BLK * h + ROWS)
                    put("dve", lambda e, i, rows=rows, h=h, pairs=pairs: e.tensor_copy(
                        diag[n][rows, pairs, :, BLK * h:BLK * h + BLK],
                        stack[frm][rows, pairs, :].rearrange("p a (b c) -> p a b c", c=BLK)),
                        wait=[f"stack {frm}", f"diag {n} read"], done=f"diag {n}{g}")
                pg.marks[f"stack {frm} copied"] = pg.marks[f"diag {n}{g}"]
                yield

        def values(a, n, w):
            for half in range(2):
                ps, read = bank()
                for k in range(NB // 2):
                    c = 1 + BLK * (k + half * NB // 2)
                    keys = xnT[n][:, c:c + BLK]
                    for h in range(2):
                        put("pe", lambda e, i, k=k, h=h, keys=keys, ps=ps: e.matmul(
                            ps[BLK * h:BLK * h + BLK, P * k:P * k + P], keys, w, start=True, stop=True),
                            wait=[read, f"xnT{n}"], done=f"v{a}" if k == NB // 2 - 1 and h == 1 else None)
                pg.marks[f"xnT{n} read"] = pg.marks[f"v{a}"]
                for h in range(2):
                    r = slice(BLK * h, BLK * h + BLK)
                    put("act", lambda e, i, r=r, h=h, half=half, ps=ps: e.activation(
                        vals[a][r, NB // 2 * half:NB // 2 * (half + 1), :, 16 * h:16 * h + D],
                        ps[r, :].rearrange("p (b a h d) -> p b a h d", b=NB // 2, a=PAIRS, h=2)[:, :, :, h, :], ACT.Copy),
                        wait=[f"v{a}", f"vals {a} read"], done=f"vals {a}")
                pg.marks[read] = pg.marks[f"vals {a}"]
                yield

        tokens = [[C, P], [P * C, NT], [1, C]]

        def start_of(b):
            return lambda e, i: b * T * C if isinstance(i, int) else e.snap(i * (T * C) + b * T * C)

        def prepare_front(b):
            put("sp", lambda e, at: e.dma_start(xs["in"][:, :, :], bass.AP(x.tensor, at, tokens)), first=start_of(b),
                wait=["xn1"], done="x loaded", dma="x")
            yield
            yield
            yield from layernorm("1", xs["in"], "x loaded")
            yield
            for n, w in (("q", M_q), ("k", M_k)):
                ps, read = bank()
                put("pe", lambda e, i, w=w, ps=ps: e.matmul(
                    ps[:, :], w[:, :], xnT["1"][:, 1:T + 1], start=True, stop=True),
                    wait=[read, "xnT1"], done=f"{n} projected")
                split(n, "a", ps, read, f"{n} projected")
                yield

        def prepare_back(b):
            restack("q", "a", "qa")
            restack("k", "a", "k")
            for _ in range(W["b0"]):
                yield
            yield from values("a", "1", M_v[:, :])
            yield from spread("qa", "qa")
            yield from row_maxima(0, max_tiles)
            yield
            yield from max_rows(0)
            yield from spread("ka", "k")
            yield from row_maxima(1, max_tiles[:AHEAD])

        max_tiles = [(step, j) for step in tiles_of_keys() for j in range(0, GROUP, 2 if step[0][0] == NB // 2 else 1)]

        def row_maxima(g, tiles):
            for step, j in tiles:
                half = step[0][0] == NB // 2
                ps, read = bank()
                if half:
                    todo = [(j, NB // 2 - 1, 0), (j + 1, NB // 2 - 1, BANK // 2)]
                elif len(step) == 2:
                    i1 = NB - 1 - step[0][0]
                    todo = [(j, i1, 0), (j, step[0][0] - 1, BLK * (i1 + 1))]
                else:
                    todo = [(j, NB - 1, 0)]
                for j_, q, at in todo:
                    pr = GROUP * g + j_
                    put("pe", lambda e, i, pr=pr, q=q, at=at, ps=ps: e.matmul(
                        ps[:, at:at + BLK * (q + 1)], diag["qa"][:, pr, q, :], stack["k"][:, pr, 0:BLK * (q + 1)],
                        start=True, stop=False), wait=[read, f"diag qa{g}", "stack k"])
                    put("pe", lambda e, i, q=q, at=at, ps=ps: e.matmul(
                        ps[:, at + BLK * q:at + BLK * (q + 1)], ident_b[:, :], mask[:, :], start=False, stop=True),
                        done="raw scores")
                for j_, q, at in todo[:1] if half else todo:
                    c, n = j_ * NB + q, 2 if half else 1
                    put("dve", lambda e, i, c=c, q=q, at=at, ps=ps, n=n: e.tensor_reduce(
                        rowmax[g][:, c:c + NB * (n - 1) + 1:NB],
                        ps[:, at:at + n * BLK * (q + 1)].rearrange("p (n c) -> p n c", n=n), axis=AX.X, op=ALU.max),
                        wait=["raw scores", f"rowmax{g} read"], done=f"rowmax{g}")
                pg.marks[read] = pg.marks[f"rowmax{g}"]
                pg.marks["stack k read"] = pg.marks["diag qa read"] = pg.marks["raw scores"]
                yield

        def max_rows(g):
            ps, read = bank()
            n, mp, mr = GROUP * NB, mparts[g], mrest[g]
            put("pe", lambda e, i: e.transpose(ps[:, 0:P], rowmax[g][:, :], ident[:, :]),
                wait=[read, f"rowmax{g}"], done=f"rowmax{g} read")
            put("act", lambda e, i: e.activation(mp[:, 0, :], ps[0:n, 0:P], ACT.Copy, scale=-1.0),
                wait=[f"rowmax{g} read", f"max rows{g}"], done="max part0")
            put("dve", lambda e, i: e.scalar_tensor_tensor(mr[:, :], ps[0:n, 0:P], -1.0, mp[:, 0, :], ALU.mult, ALU.subtract),
                wait=["max part0", f"rowmax{g} read"], done="max rest")
            pg.marks[read] = pg.marks["max rest"]
            put("dve", lambda e, i: e.tensor_copy(mp[:, 1, :], mr[:, :]), wait=["max rest", f"max rows{g}"], done="max part1")
            put("dve", lambda e, i: e.tensor_tensor(mp[:, 2, :], mr[:, :], mp[:, 1, :], ALU.subtract),
                wait=["max part1"], done="max part2")
            for h in range(2):
                for part in range(3):
                    row = BLK * h + ROWS + part
                    put("sp", lambda e, i, h=h, part=part, row=row: e.dma_start(
                        stack["qa"][row:row + 1, GROUP * g:GROUP * g + GROUP, :], mp[:, part, BLK * h:BLK * h + BLK]),
                        wait=["max part0", "max part2", "stack qa read", "stack qa copied"], done=f"max rows{g}", dma=f"max{g}")
            yield

        def scores(a, scale, g, step, u):
            q, kd = stack["q" + a], diag["k" + a]
            ready = [f"stack q{a}", f"diag k{a}{g}"] + ([f"max rows{g}"] if a == "a" else [])
            half = step[0][0] == NB // 2
            n, t = unit[0], unit[0] % 2
            unit[0] += 1
            placed = []
            for k in range(2):
                todo = ([(2 * k + z, NB // 2, z * BANK // 2) for z in range(2)] if half
                        else [(2 * u + k, blk, at) for blk, at in step])
                for j, blk, at in todo:
                    pair, width = GROUP * g + j, T - BLK * blk
                    put("pe", lambda e, i, k=k, at=at, width=width, pair=pair, blk=blk: e.matmul(
                        score[t][:, k, at:at + width], kd[:, pair, blk, :], q[:, pair, BLK * blk:T],
                        start=True, stop=a == "b"),
                        wait=[f"score{t} read", *ready], done=f"scores{t}")
                    if a == "a":
                        put("pe", lambda e, i, k=k, at=at: e.matmul(
                            score[t][:, k, at:at + BLK], ident_b[:, :], mask_t[:, :], start=False, stop=True),
                            done=f"scores{t}")
                    placed.append((j, blk, n % NPROB, k, at))
            pr = prob[n % NPROB]
            put("act", lambda e, i: e.activation(pr[:, :, :], score[t][:, :, :], ACT.Exp, scale=scale),
                wait=[f"scores{t}", f"prob{n % NPROB} read"], done=f"score{t} read")
            if a == "a":
                pg.marks[f"prob{n % NPROB}"] = pg.marks[f"score{t} read"]
                return placed
            blocks = 1 if step[0][0] == 0 else 2
            gap = BANK // 2 if half else T - BLK * step[0][0]
            start = bass.AP(pr, 0, [[2 * BANK, P], [BANK, 2], [gap, blocks], [1, BLK]])
            alone(lambda e, i: e.tensor_tensor(
                start, start, seen[:, :].rearrange("p (a b c) -> p a b c", a=1, b=1).to_broadcast([P, 2, blocks, BLK]),
                ALU.mult), [f"score{t} read"], f"prob{n % NPROB}")
            return placed

        def weigh(a, g, blk, tiles):
            for j, slot, k, at in tiles:
                put("pe", lambda e, i, j=j, slot=slot, k=k, at=at: e.matmul(
                    acc[32 * j:32 * j + 32, BLK * blk:T], vals[a][:, blk, GROUP * g + j, :],
                    prob[slot][:, k, at:at + T - BLK * blk], start=blk == 0, stop=blk == NB // 2),
                    wait=[f"prob{slot}", "acc read", f"vals {a}"], done=f"prob{slot} read")
                pg.marks[f"{a} summed"] = pg.marks[f"prob{slot} read"]
            if blk == NB // 2:
                put("act", lambda e, i: e.activation(outT[a][g][:, :], acc[:, :], ACT.Copy),
                    wait=[f"{a} summed", f"outT{a}{g} read"], done="acc read")
                pg.marks[f"outT{a}{g}"] = pg.marks["acc read"]

        def attend(a, scale):
            behind = []
            for g, step in [(g, step) for g in range(GROUPS) for step in tiles_of_keys()] + [(None, None)]:
                placed = []
                for u in range(1 if step and step[0][0] == NB // 2 else 2):
                    if step:
                        placed += scores(a, scale, g, step, u)
                        yield
                    if behind:
                        weigh(a, *behind.pop(0))
                        yield
                while behind:
                    weigh(a, *behind.pop(0))
                    yield
                behind = [(g, blk, [(j, *p) for j, b, *p in placed if b == blk]) for blk in sorted({p[1] for p in placed})]
            pg.marks[f"vals {a} read"] = pg.marks[f"stack q{a} read"] = pg.marks[f"diag k{a} read"] = pg.marks[f"{a} summed"]

        def normalise(a, g):
            ps, read = bank()
            src = outT[a][g]
            for k in range(NT):
                put("pe", lambda e, i, k=k: e.transpose(
                    ps[:, P * k:P * k + P], src[:, P * k:P * k + P], ident[:, :]),
                    wait=[read, f"outT{a}{g}"], done=f"outT{a}{g} read" if k == NT - 1 else None)
            heads = ps[:, :].rearrange("p (k h c) -> p k h c", k=NT, c=16)
            put("dve", lambda e, i: e.reciprocal(
                rden[a][g][:, :].rearrange("p (k h) -> p k h", k=NT), heads[:, :, :, D]),
                wait=[f"outT{a}{g} read"], done=f"rden{a}{g}")
            w = 2 * GROUP * D
            put("dve", lambda e, i: e.tensor_tensor(
                y[a][:, :, w * g:w * g + w].rearrange("p k (h d) -> p k h d", d=D), heads[:, :, :, 0:D],
                rden[a][g][:, :].rearrange("p (k h o) -> p k h o", k=NT, o=1).to_broadcast([P, NT, 2 * GROUP, D]),
                ALU.mult), wait=[f"rden{a}{g}", f"y{a} read"], done=f"y{a}")
            pg.marks[read] = pg.marks[f"y{a}"]
            yield

        def feed_forward(n, src, dst, dst_free, result):
            f = ffn
            now, before = xnT[n][:, 1:T + 1], xnT[n][:, 0:T]
            alone(lambda e, i: e.tensor_tensor(f["diff"][:, :], now, before, ALU.subtract),
                [f"xnT{n}", "mixed"], f"xnT{n} diff read")
            yield
            for k, b in enumerate(("xk", "xr")):
                put("dve", lambda e, i, k=k, b=b: e.scalar_tensor_tensor(
                    f[b][:, :], f["diff"][:, :], mu[:, 1 - k:2 - k], before, ALU.mult, ALU.add),
                    wait=[f"xnT{n} diff read", f"{b} read"], done=b)
            pg.marks["mixed"] = pg.marks[f"xnT{n} read"] = pg.marks["xr"]
            yield
            ps, read = bank()
            put("pe", lambda e, i, ps=ps: e.matmul(ps[:, :], T_k[:, :], f["xk"][:, :], start=True, stop=True),
                wait=[read, "xk"], done="xk read")
            put("act", lambda e, i, ps=ps: e.activation(f["act"][:, :], ps[:, :], ACT.Relu),
                wait=["xk read", "act read"], done="relu")
            pg.marks[read] = pg.marks["relu"]
            alone(lambda e, i: e.tensor_tensor(f["act"][:, :], f["act"][:, :], f["act"][:, :], ALU.mult),
                ["relu", "act read"], "act")
            yield
            ps, read = bank()
            for k in range(NT):
                put("pe", lambda e, i, k=k, ps=ps: e.matmul(ps[:, P * k:P * k + P], f["xr"][:, P * k:P * k + P], T_r[:, :],
                                                            start=True, stop=True),
                    wait=[read, "xr"], done="xr read" if k == NT - 1 else None)
            put("act", lambda e, i, ps=ps: e.activation(f["gate"][:, :], ps[:, :], ACT.Tanh, scale=0.5),
                wait=["xr read", "prod"], done="gate")
            pg.marks[read] = pg.marks["gate"]
            yield
            ps, read = bank()
            for k in range(NT):
                put("pe", lambda e, i, k=k, ps=ps: e.matmul(ps[:, P * k:P * k + P], f["act"][:, P * k:P * k + P], T_v[:, :],
                                                            start=True, stop=True),
                    wait=[read, "act"], done="act read" if k == NT - 1 else None)
            put("dve", lambda e, i, ps=ps: e.scalar_tensor_tensor(f["prod"][:, :], f["gate"][:, :], 1.0, ps[:, :],
                                                                  ALU.add, ALU.mult),
                wait=["act read", "gate", "prod read"], done="prod")
            pg.marks[read] = pg.marks["prod"]
            alone(lambda e, i: e.tensor_tensor(dst[:, :, :], src[:, :, :],
                                                     f["prod"][:, :].rearrange("p (k c) -> p k c", k=NT), ALU.add),
                wait=["prod", *dst_free], done=result)
            pg.marks["prod read"] = pg.marks[result]
            yield

        def middle_front(b):
            put("sp", lambda e, at: e.dma_start(xs["again"][:, :, :], bass.AP(x.tensor, at, tokens)), first=start_of(b),
                wait=["x_a"], done="x loaded again", dma="again")
            yield from normalise("a", 1)
            alone(lambda e, i: e.tensor_tensor(xs["a"][:, :, :], xs["again"][:, :, :], y["a"][:, :, :], ALU.add),
                ["ya", "x_ffn", "xn2", "x loaded again"], "x_a")
            pg.marks["ya read"] = pg.marks["x_a"]
            yield
            yield
            yield from layernorm("2", xs["a"], "x_a")
            yield from feed_forward("2", xs["a"], xs["ffn"], ["x_ffn kept", "xn3"], "x_ffn")

        def middle_back():
            yield from layernorm("3", xs["ffn"], "x_ffn")
            yield
            for half in range(2):
                ps, read = bank()
                for k in range(2):
                    tile = 2 * half + k
                    put("pe", lambda e, i, k=k, tile=tile, ps=ps: e.matmul(
                        ps[:, 2 * C * k:2 * C * (k + 1)], xnT["3"][:, 1 + P * tile:1 + P * (tile + 1)],
                        w_qk[:, :, :].rearrange("p a c -> p (a c)"), start=True, stop=True),
                        wait=[read, "xnT3"], done="qk projected" if k else None)
                two = slice(2 * half, 2 * half + 2)
                for to, func, free in ((qk, ACT.Square, "qk read"), (raw, ACT.Copy, "qk")):
                    put("act", lambda e, i, two=two, ps=ps, to=to, func=func: e.activation(
                        to[:, two, :, :].rearrange("p k a c -> p k (a c)"), ps[:, :].rearrange("p (k c) -> p k c", k=2), func),
                        ["qk projected", free], "raw qk")
                pg.marks[read] = pg.marks["raw qk"]
                w = 2 * 2 * HEADS
                put("dve", lambda e, i, two=two, half=half: e.tensor_reduce(
                    ssum[:, w * half:w * (half + 1)].rearrange("p (k n) -> p k n", k=2),
                    qk[:, two, :, :].rearrange("p k a (h d) -> p k (a h) d", d=D), axis=AX.X, op=ALU.add),
                    wait=["raw qk", "rnorm"], done="norms2")
                yield
            pg.marks["xnT3 read"] = pg.marks["qk projected"]
            yield from rsqrt_of_ssum()
            yield from values("b", "3", w_v[:, :])
            for half in range(2):
                two = slice(2 * half, 2 * half + 2)
                w = 2 * 2 * HEADS
                put("dve", lambda e, i, two=two, half=half: e.tensor_tensor(
                    qk[:, two, :, :].rearrange("p k a (d h) -> p (k a) h d", d=D),
                    raw[:, two, :, :].rearrange("p k a (h d) -> p (k a) h d", d=D),
                    rnorm[:, w * half:w * (half + 1)].rearrange("p (k h o) -> p k h o", k=4, o=1).to_broadcast([P, 4, HEADS, D]),
                    ALU.mult), wait=["rnorm", "raw qk", "qk read"], done="qk")
            yield
            yield
            for a, n in enumerate("qk"):
                ps, read = bank()
                for k in range(NT):
                    put("pe", lambda e, i, k=k, a=a, ps=ps: e.transpose(ps[:, P * k:P * k + P], qk[:, k, a, :], ident[:, :]),
                        wait=[read, "qk"], done=f"{n} turned" if k == NT - 1 else None)
                split(n, "b", ps, read, f"{n} turned")
                yield
            pg.marks["qk read"] = pg.marks["k turned"]
            yield
            restack("k", "b", "k")
            restack("q", "b", "qb")
            yield

        def rsqrt_of_ssum():
            put("dve", lambda e, i: e.tensor_scalar(ssum[:, :], ssum[:, :], 1e-24, None, ALU.max),
                wait=["norms2"], done="norms2 kept up")
            put("dve", lambda e, i: e.tensor_scalar(rnorm[:, :].bitcast(mybir.dt.int32), ssum[:, :].bitcast(mybir.dt.int32),
                                                    -0.5, float(0x5f3759df), ALU.mult, ALU.add),
                wait=["norms2 kept up", "qk"], done="rnorm")
            for _ in range(3):
                put("dve", lambda e, i: e.scalar_tensor_tensor(step_r[:, :], rnorm[:, :], -0.5, rnorm[:, :], ALU.mult, ALU.mult),
                    wait=["rnorm"], done="rnorm step")
                put("dve", lambda e, i: e.tensor_tensor(step_r[:, :], step_r[:, :], ssum[:, :], ALU.mult),
                    wait=["rnorm step"], done="rnorm step")
                put("dve", lambda e, i: e.scalar_tensor_tensor(rnorm[:, :], step_r[:, :], 1.5, rnorm[:, :], ALU.add, ALU.mult),
                    wait=["rnorm step"], done="rnorm")
            yield

        def finish(b):
            for g in range(GROUPS):
                yield from normalise("b", g)
            yield
            ps, read = bank()
            for k in range(NT):
                put("pe", lambda e, i, k=k, ps=ps: e.transpose(ps[:, P * k:P * k + P], y["b"][:, k, :], ident[:, :]),
                    wait=[read, "yb"], done="yb read" if k == NT - 1 else None)
            put("act", lambda e, i, ps=ps: e.activation(yT[:, :], ps[:, :], ACT.Copy), wait=["yb read", "yT read"], done="yT")
            pg.marks[read] = pg.marks["yT"]
            yield
            yield
            ps, read = bank()
            for k in range(NT):
                put("pe", lambda e, i, k=k, ps=ps: e.matmul(ps[:, P * k:P * k + P], yT[:, P * k:P * k + P], w_ob[:, :],
                                                            start=True, stop=True),
                    wait=[read, "yT"], done="yT read" if k == NT - 1 else None)
            put("dve", lambda e, i, ps=ps: e.tensor_tensor(xs["b"][:, :, :], ps[:, :].rearrange("p (k c) -> p k c", k=NT),
                                                           xs["kept"][:, :, :], ALU.add),
                wait=["yT read", "x_ffn kept", "x_out", "xn4"], done="x_b")
            pg.marks[read] = pg.marks["x_b"]
            yield
            yield from layernorm("4", xs["b"], "x_b")
            yield from feed_forward("4", xs["b"], xs["out"], ["stored"], "x_out")
            put("sp", lambda e, at: e.dma_start(bass.AP(out.tensor, at, tokens), xs["out"][:, :, :]), first=start_of(b),
                wait=["x_out"], done="stored", dma="out")
            yield

        def keep():
            put("sp", lambda e, i: e.dma_start(xs["kept"][:, :, :], xs["ffn"][:, :, :]),
                wait=["x_ffn", "x_b"], done="x_ffn kept", dma="keep")
            yield

        SLOTS = 36
        AHEAD = W["ahead"]

        def weave(main, sides):
            for slot in range(SLOTS):
                if main:
                    next(main, None)
                for gen, n, first, last in sides:
                    due = lambda at: min(n, max(0, (at - first) * n // (last - first)))
                    for _ in range(due(slot + 1) - due(slot)):
                        next(gen, None)
            for gen, n, *_ in [(main or iter(()), 0), *sides]:
                left = sum(1 for _ in gen)
                assert not left, f"{gen.__name__} has {left} steps more than {n}"

        def iteration(t):
            live = lambda b: 0 <= b < B
            sides = []
            if live(t):
                sides.append((row_maxima(1, max_tiles[AHEAD:]), len(max_tiles) - AHEAD, *W["max"]))
                sides.append((max_rows(1), 1, *W["rows"]))
            if live(t - 1):
                sides.append((middle_back(), 18, *W["mb"]))
            if live(t - 2):
                sides.append((finish(t - 2), 19, *W["fin"]))
            if live(t + 1):
                sides.append((prepare_front(t + 1), 9, *W["pf"]))
            if live(t - 1):
                sides.append((keep(), 1, *W["keep"]))
                sides.append((spread("kb", "k"), 2, *W["kb"]))
            if live(t):
                sides.append((normalise("a", 0), 1, *W["na"]))
            weave(attend("a", 1.0) if live(t) else None, sides)
            sides = []
            if live(t):
                sides.append((middle_front(t), 12, *W["mf"]))
            if live(t + 1):
                sides.append((prepare_back(t + 1), 27 + AHEAD + W["b0"], *W["pb"]))
            weave(attend("b", 8.0) if live(t - 1) else None, sides)
            ring[0] += -ring[0] % 3

        pieces = []
        setup()
        for gen in (prepare_front(0), prepare_back(0)):
            for _ in gen:
                pass
        for t in range(3):
            iteration(t)
        pieces.append((pg.cut(), 1, None))
        first, last = 3, B - 2
        assert last > first

        def shape(items, counts):
            return [[(s.sem.name, v - counts[s]) for s, v in waits] for waits, *_ in items]

        kept = None
        for t in range(first, last + 1):
            before, r0, u0 = pg.counts(), ring[0], unit[0]
            iteration(t)
            piece = pg.cut()
            assert (ring[0] - r0) % 3 == 0 and (unit[0] - u0) % 2 == 0 and (unit[0] - u0) % NPROB == 0
            grow = {s: n - before[s] for s, n in pg.counts().items()}
            form = {k: shape(v, before) for k, v in piece.items()}
            if kept is None:
                kept = (piece, grow, form)
            assert kept[1] == grow and kept[2] == form, "turns of the loop differ"
        pieces.append((kept[0], last - first + 1, kept[1]))
        for t in range(last + 1, B + 2):
            iteration(t)
        put("sp", lambda e, i: e.nop(), wait=["stored"])
        pieces.append((pg.cut(), 1, None))

        block = ctx.enter_context(nc.Block())

        def run(name, eng):
            for items, count, grow in pieces:
                if count == 1:
                    emit(eng, items[name])
                else:
                    with eng.Fori(0, count) as i:
                        emit(eng, items[name], i, grow)

        @block.sync
        def _(eng):
            run("sp", eng)

        @block.gpsimd
        def _(eng):
            run("pool", eng)

        @block.scalar
        def _(eng):
            run("act", eng)

        @block.vector
        def _(eng):
            run("dve", eng)

        @block.tensor
        def _(eng):
            run("pe", eng)


_NAMES = ["L0_attn_a_x", "L0_attn_a_W_dq", "L0_attn_a_W_uq", "L0_attn_a_W_dkv", "L0_attn_a_W_uk", "L0_attn_a_W_uv",
          "L0_attn_a_W_o", "L0_attn_b_Wq", "L0_attn_b_Wk", "L0_attn_b_Wv", "L0_attn_b_Wo",
          "L0_ffn_W_r", "L0_ffn_W_k", "L0_ffn_W_v", "L0_ffn_mu_r", "L0_ffn_mu_k"]


def kernel(**inputs):
    import concourse.bacc as bacc
    from concourse.bass_utils import run_bass_kernel_spmd

    nc = bacc.Bacc("TRN2", target_bir_lowering=False, num_devices=1)
    arrays, args = {}, []
    for name in _NAMES:
        a = np.ascontiguousarray(inputs[name])
        arrays["in_" + name] = a
        args.append(nc.dram_tensor("in_" + name, a.shape, mybir.dt.from_np(a.dtype), kind="ExternalInput").ap())
    shape = inputs["L0_attn_a_x"].shape
    args.append(nc.dram_tensor("out_0", shape, F32, kind="ExternalOutput").ap())
    build(nc, *args)
    r = run_bass_kernel_spmd(nc, [arrays], core_ids=[0])
    return r.results[0]["out_0"]
```

```python
import numpy as np
import concourse.bass as bass
from concourse import mybir
from contextlib import ExitStack
from itertools import chain, islice

F32, BF16 = mybir.dt.float32, mybir.dt.bfloat16
ALU, ACT, AX = mybir.AluOpType, mybir.ActivationFunctionType, mybir.AxisListType

P = 128
HEADS = 16
PAIRS = HEADS // 2
GROUP = 4
GROUPS = PAIRS // GROUP
BLK = 64
BANK = 512
ROWS = 48
BIG = -3.0e37
EPS = 1e-5
STACK = [(0, (0, 0, 0), (0, 1, 2)), (3, (1, 1), (0, 1)), (5, (2,), (0,))]
PRODUCTS = 6


class Lane:

    def __init__(self, sem, by=1):
        self.sem, self.by, self.count, self.items, self.seen = sem, by, 0, [], {}

    def mark(self):
        self.count += self.by
        return (self, self.count)


class Program:

    def __init__(self, engines, dmas):
        self.lanes, self.dmas, self.marks = engines, dmas, {}

    def put(self, lane, make, wait=(), done=None, dma=None, first=None):
        line, waits = self.lanes[lane], []
        for name in wait:
            m = self.marks.get(name)
            if m and line.seen.get(m[0], 0) < m[1]:
                line.seen[m[0]] = m[1]
                waits.append(m)
        inc = None
        if done is not None:
            source = self.dmas[dma] if dma else line
            self.marks[done] = source.mark()
            inc = (source.sem, source.by)
        line.items.append((waits, make, inc, first))

    def cut(self):
        piece = {k: v.items for k, v in self.lanes.items()}
        for v in self.lanes.values():
            v.items, v.seen = [], {}
        return piece

    def counts(self):
        return {x: x.count for x in [*self.lanes.values(), *self.dmas.values()]}


def emit(engine, items, i=0, grow=None):
    for waits, make, inc, first in items:
        arg = first(engine, i) if first else i
        values = [i * grow[source] + value if grow else value for source, value in waits]
        for value in values if grow else ():
            engine.compute_val(value)
        for (source, _), value in zip(waits, values):
            engine.wait_ge(source.sem, value)
        made = make(engine, arg)
        if inc:
            made.then_inc(*inc)


def tiles_of_keys():
    n = BANK // BLK
    return [[(0, 0)]] + [[(i, 0), (n - i, BANK - BLK * i)] for i in range(1, n // 2)] + [[(n // 2, 0)]]


def build(nc, x, wdq, wuq, wdkv, wuk, wuv, wo_a, wq, wk, wv, wo_b, wr, wkf, wvf, mur, muk, out):
    B, T, C = x.shape
    NT = T // P
    NB = T // BLK
    D = C // HEADS
    QL, KVL = wdq.shape[0], wdkv.shape[0]
    NPROB = 4

    ctx = ExitStack()
    with ctx:
        def sb(name, shape, dt=F32):
            return ctx.enter_context(nc.sbuf_tensor(name, shape, dt))

        def sem(name):
            return ctx.enter_context(nc.semaphore(name))

        ident = sb("ident", [P, P])
        ident_b = sb("ident_b", [P, P], BF16)
        ones_b = sb("ones_b", [3, PAIRS * BLK], BF16)
        carrier = sb("carrier", [P, 6])
        mask = sb("mask", [P, BLK], BF16)
        mask_t = sb("mask_t", [P, BLK], BF16)
        minus_half = sb("minus_half", [P, 1])
        w_in = {n: sb("raw_" + n, list(a.shape)) for n, a in
                dict(dq=wdq, uq=wuq, dkv=wdkv, uk=wuk, uv=wuv, o=wo_a, r=wr, k=wkf, v=wvf).items()}
        w_qk = sb("w_qk", [P, 2, C])
        w_v = sb("w_v", [P, C])
        w_ob = sb("w_ob", [P, C])
        mu = sb("mu", [P, 2])
        T_uq = sb("T_uq", [QL, C])
        T_o = sb("T_o", [P, C])
        T_r = sb("T_r", [P, C])
        T_k = sb("T_k", [P, C])
        T_v = sb("T_v", [P, C])
        M_q = sb("M_q", [P, C])
        M_qT = sb("M_qT", [P, C])
        k_effT = sb("k_effT", [KVL, C])
        v_eff = sb("v_eff", [KVL, C])
        M_k = sb("M_k", [P, C])
        M_v = sb("M_v", [P, C])
        xs = {n: sb("x_" + n, [P, NT, C]) for n in ("in", "again", "a", "ffn", "kept", "b", "out")}
        stats = {n: sb(f"stats_{n}", [P, NT, 6]) for n in ("1", "2", "3", "4")}
        mv = {n: sb(f"mv_{n}", [P, NT, 2]) for n in stats}
        rstd = {n: sb(f"rstd_{n}", [P, NT]) for n in stats}
        xn = {n: sb(f"xn_{n}", [P, NT, C]) for n in stats}
        xnT = {n: sb(f"xnT_{n}", [P, T + 1]) for n in stats}
        ffn = {n: sb("ffn_" + n, [P, T]) for n in ("diff", "xr", "xk", "act", "gate", "prod")}
        parts = {n: sb("parts_" + n, [P, 3, T], BF16) for n in "qk"}
        rest = {n: sb("rest_" + n, [P, T]) for n in parts}
        stack = {n: sb("stack_" + n, [P, PAIRS, T], BF16) for n in ("qa", "qb", "k")}
        diag = {n: sb("diag_" + n, [P, PAIRS, NB, P], BF16) for n in ("qa", "ka", "kb")}
        vals = {n: sb("vals_" + n, [P, NB, PAIRS, 32]) for n in "ab"}
        rowmax = [sb(f"rowmax{g}", [P, GROUP * NB]) for g in range(GROUPS)]
        mparts = [sb(f"mparts{g}", [P, P // (GROUP * NB), GROUP * NB], BF16) for g in range(GROUPS)]
        mrest = [sb(f"mrest{g}", [P, GROUP * NB]) for g in range(GROUPS)]
        mturned = [sb(f"mturned{g}", [P, P], BF16) for g in range(GROUPS)]
        prob = [sb(f"prob{i}", [P, 2, BANK]) for i in range(NPROB)]
        outT = {n: [sb(f"outT_{n}{g}", [P, T]) for g in range(GROUPS)] for n in "ab"}
        rden = {n: [sb(f"rden_{n}{g}", [P, NT * 2 * GROUP]) for g in range(GROUPS)] for n in "ab"}
        y = {n: sb("y_" + n, [P, NT, C]) for n in "ab"}
        yT = sb("yT", [P, T])
        raw = sb("raw", [P, NT, 2, C])
        qk = sb("qk", [P, NT, 2, C])
        ssum = sb("ssum", [P, NT * 2 * HEADS])
        rnorm = sb("rnorm", [P, NT * 2 * HEADS])
        step_r = sb("step_r", [P, NT * 2 * HEADS])

        def pb(name, shape, dt=F32):
            return ctx.enter_context(nc.psum_tensor(name, shape, dt))

        score = [pb(f"score{i}", [P, 2, BANK]) for i in range(2)]
        acc = pb("acc", [P, BANK])
        misc = [pb(f"misc{i}", [P, BANK]) for i in range(3)]

        scratch = {n: nc.dram_tensor("scratch_" + n, (PRODUCTS, P, T), BF16, kind="Internal").ap()
                   for n in ("qa", "ka", "qb", "kb")}

        lanes = {n: Lane(sem("s_" + n)) for n in ("pe", "act", "dve", "pool", "sp")}
        dmas = {n: Lane(sem("s_dma_" + n), 16) for n in
                ["w", "x", "again", "keep", "out", "max0", "max1", "ones"]
                + ["out_" + n for n in scratch] + ["in_" + n for n in scratch]}
        pg = Program(lanes, dmas)
        put = pg.put

        def alone(make, wait, done):
            put("pool", make, wait=["pool before", *wait], done=done)
            pg.marks["pool before"] = pg.marks[done]

        SLOTS = 36
        PLAN = {
            "row_maxima": [1, 2, 3, 4, 5, 6, 7, 8, 9, 10, 11],
            "max_rows": [13, 14],
            "middle_back": [1, 3, 5, 7, 9, 10, 10, 12, 13, 15, 17, 19],
            "finish": [4, 6, 10, 13, 15, 19, 21, 23, 24, 26, 28, 30, 32],
            "prepare_front": [10, 14, 21, 21, 25, 27],
            "keep": [24],
            "spread": [33, 34],
            "normalise": [27],
            "prepare_stacks": [31, 35],
            "middle_front": [1, 3, 7, 13, 15, 17, 19, 21, 23, 24],
            "values": [2, 2],
            "prepare_back": [3, 4, 5, 6, 7, 8, 9, 10, 11, 12, 13, 14, 15, 16, 17, 18, 19, 20, 21, 22, 23, 24, 25, 26,
                             27, 28, 29, 30, 31, 34, 35],
        }

        ring, unit = [0], [0]

        def bank():
            k = ring[0] % 3
            ring[0] += 1
            return misc[k], f"misc{k} read"

        def setup():
            front = prepare_front(0)
            next(front)
            loads = [(w_in["dq"][:, :], wdq), (w_in["uq"][:, :], wuq), (w_in["dkv"][:, :], wdkv), (w_in["uk"][:, :], wuk),
                     (w_in["uv"][:, :], wuv), (w_in["o"][:, :], wo_a), (w_in["r"][:, :], wr), (w_in["k"][:, :], wkf),
                     (w_in["v"][:, :], wvf), (w_qk[:, 0, :], wq), (w_qk[:, 1, :], wk), (w_v[:, :], wv), (w_ob[:, :], wo_b),
                     (mu[:, 0:1], mur.rearrange("(c o) -> c o", o=1)), (mu[:, 1:2], muk.rearrange("(c o) -> c o", o=1))]
            for dst, src in loads:
                put("sp", lambda e, i, d=dst, s=src: e.dma_start(d, s), done="weights", dma="w")
            put("dve", lambda e, i: e.memset(minus_half[:, :], -0.5), done="ones")
            put("dve", lambda e, i: e.memset(ones_b[:, :], 1.0), done="ones")
            for t in xnT.values():
                put("dve", lambda e, i, t=t: e.memset(t[:, 0:1], 0.0), done="ones")
            for t in mparts:
                put("dve", lambda e, i, t=t: e.memset(t[:, :, :], 0.0), done="ones")
            for m in (ident, ident_b):
                alone(lambda e, i, m=m: e.memset(m[:, :], 0.0), [], "ident")
                alone(lambda e, i, m=m: e.affine_select(
                    out=m[:, :], in_=m[:, :], compare_op=ALU.not_equal, fill=1.0, base=0,
                    pattern=[[-1, P]], channel_multiplier=1), [], "ident")
            put("pe", lambda e, i: e.nop(), wait=["ident"])
            put("pool", lambda e, i: e.nop(), wait=["ones"])
            for _ in range(3):
                next(front)

            for m, sign in ((mask, 1), (mask_t, -1)):
                alone(lambda e, i, m=m: e.memset(m[:, :], 0.0), [], "mask")
                for h in range(2):
                    alone(lambda e, i, m=m[BLK * h:BLK * h + BLK, :], sign=sign: e.affine_select(
                        out=m, in_=m, compare_op=ALU.is_ge, fill=BIG, base=0, pattern=[[-sign, BLK]],
                        channel_multiplier=sign), [], "mask")
            for t in (vals["a"], vals["b"]):
                alone(lambda e, i, t=t: e.memset(t[:, :, :, :], 0.0), [], "vals ones")
                for h in range(2):
                    column = t[BLK * h:BLK * h + BLK, :, :, 16 * h + D:16 * h + D + 1]
                    alone(lambda e, i, column=column: e.memset(column, 1.0), [], "vals ones")

            def whole(t):
                names = " ".join("abc"[:len(t.shape) - 1])
                return t[(slice(None),) * len(t.shape)].rearrange(f"p {names} -> p ({names})").bitcast(F32)

            for t in (stack["qa"], stack["k"], diag["qa"], diag["ka"]):
                put("dve", lambda e, i, t=t: e.memset(whole(t), 0.0), done="zeroed")
            for t in (stack["qb"], diag["kb"]):
                alone(lambda e, i, t=t: e.memset(whole(t), 0.0), [], "zeroed for b")

            def product(dst, lhsT, rhs, wait, name, scale=1.0, transpose=False, dims_first=False):
                ps, read = bank()
                m, n = dst.shape[0], dst.shape[-1]
                if transpose:
                    k = lhsT.shape[0]
                    put("pe", lambda e, i: e.transpose(ps[0:m, 0:n], lhsT, ident[0:k, 0:k]),
                        wait=[read, "weights", "ident", *wait], done=name + " product")
                else:
                    put("pe", lambda e, i: e.matmul(ps[0:m, 0:n], lhsT, rhs, start=True, stop=True),
                        wait=[read, "weights", *wait], done=name + " product")
                to, of = dst, ps[0:m, 0:n]
                if dims_first:
                    to, of = to.rearrange("c (d h) -> c h d", d=D), of.rearrange("c (h d) -> c h d", d=D)
                put("act", lambda e, i: e.activation(to, of, ACT.Copy, scale=scale),
                    wait=[name + " product"], done=name)
                pg.marks[read] = pg.marks[name]

            product(T_uq[:, :], w_in["uq"][:, :], None, [], "T_uq", transpose=True)
            product(T_o[:, :], w_in["o"][:, :], None, [], "T_o", transpose=True)
            product(M_qT[:, :], T_uq[:, :], w_in["dq"][:, :], ["T_uq"], "M_qT")
            product(M_q[:, :], w_in["dq"][:, :], T_uq[:, :], ["T_uq"], "M_q", scale=float(D) ** -0.5, dims_first=True)
            product(k_effT[:, :], w_in["uk"][:, :], M_qT[:, :], ["M_qT"], "k_effT")
            product(v_eff[:, :], w_in["uv"][:, :], T_o[:, :], ["T_o"], "v_eff")
            product(M_k[:, :], w_in["dkv"][:, :], k_effT[:, :], ["k_effT"], "M_k", dims_first=True)
            product(M_v[:, :], w_in["dkv"][:, :], v_eff[:, :], ["v_eff"], "M_v")
            for t, n in ((T_r, "r"), (T_k, "k"), (T_v, "v")):
                product(t[:, :], w_in[n][:, :], None, [], "T_" + n, transpose=True, scale=0.5 if n == "v" else 1.0)
            for lane in ("pe", "dve"):
                put(lane, lambda e, i: e.nop(), wait=["weights", "T_v", "mask", "ones"])
            for _ in front:
                pass
            for lane in ("sp", "act", "pe"):
                put(lane, lambda e, i: e.nop(), wait=["zeroed", "vals ones"])
            for _ in prepare_stacks():
                pass
            for h in range(2):
                for blk in range(NB):
                    put("sp", lambda e, i, h=h, blk=blk: e.dma_start(
                        diag["ka"][BLK * h + ROWS:BLK * h + ROWS + 3, :, blk, BLK * h:BLK * h + BLK],
                        ones_b[:, :].rearrange("p (a c) -> p a c", c=BLK)), done="ones rows", dma="ones")
            for _ in chain(values("a", "1", M_v[:, :]), prepare_back()):
                pass
            put("pe", lambda e, i: e.nop(), wait=["ones rows"])
            for lane in ("sp", "dve", "pe"):
                put(lane, lambda e, i: e.nop(), wait=["zeroed for b"])

        def layernorm(n, src, ready):
            s, m, r, o = stats[n], mv[n], rstd[n], xn[n]
            for k in range(NT):
                put("dve", lambda e, i, k=k: e.bn_stats(s[:, k, :], src[:, k, :]), wait=[ready], done=f"stats{n}")
            put("dve", lambda e, i: e.tensor_copy(carrier[:, :], s[:, NT - 1, :]), wait=[f"stats{n}"])
            for k in range(NT):
                put("dve", lambda e, i, k=k: e.bn_aggr(m[:, k, :], s[:, k, :]), done=f"mv{n}")
            put("dve", lambda e, i: e.tensor_scalar(m[:, :, 1], m[:, :, 1], EPS, None, ALU.add),
                wait=[f"mv{n}"], done=f"var{n}")
            alone(lambda e, i: e.tensor_tensor(r[:, :], m[:, :, 1], minus_half[:, 0:1].to_broadcast([P, NT]), ALU.pow),
                  [f"var{n}", f"xn{n}"], f"rstd{n}")
            yield
            for k in range(NT):
                put("dve", lambda e, i, k=k: e.tensor_scalar(o[:, k, :], src[:, k, :], m[:, k, 0:1], r[:, k:k + 1],
                                                             ALU.subtract, ALU.mult),
                    wait=[f"rstd{n}", f"xn{n} transposed"], done=f"xn{n}")
            yield
            ps, read = bank()
            for k in range(NT):
                put("pe", lambda e, i, k=k: e.transpose(ps[:, P * k:P * k + P], o[:, k, :], ident[:, :]),
                    wait=[read, f"xn{n}"], done=f"xn{n} transposed" if k == NT - 1 else None)
            put("act", lambda e, i: e.activation(xnT[n][:, 1:T + 1], ps[:, :], ACT.Copy),
                wait=[f"xn{n} transposed", f"xnT{n} read", f"xnT{n} diff read"], done=f"xnT{n}")
            pg.marks[read] = pg.marks[f"xnT{n}"]
            yield

        def split(n, a, ps, read, filled):
            p, r = parts[n], rest[n]
            put("act", lambda e, i: e.activation(p[:, 0, :], ps[:, :], ACT.Copy),
                wait=[filled, f"parts {n} written out"], done=f"{n} part0")
            put("dve", lambda e, i: e.tensor_tensor(r[:, :], ps[:, :], p[:, 0, :], ALU.subtract),
                wait=[f"{n} part0", filled, f"{n} part2"], done=f"{n} rest")
            pg.marks[read] = pg.marks[f"{n} rest"]
            put("dve", lambda e, i: e.tensor_copy(p[:, 1, :], r[:, :]),
                wait=[f"{n} rest", f"parts {n} written out"], done=f"{n} part1")
            alone(lambda e, i: e.tensor_tensor(p[:, 2, :], r[:, :], p[:, 1, :], ALU.subtract),
                [f"{n} rest", f"{n} part1", f"parts {n} written out"], f"{n} part2")
            side = 1 if n == "q" else 2
            for run in STACK:
                first, chosen = run[0], run[side]
                src = (p[:, chosen[0]:chosen[0] + 1, :].to_broadcast([P, len(chosen), T]) if chosen[0] == chosen[-1]
                       else p[:, 0:len(chosen), :])
                put("sp", lambda e, i, src=src, first=first, c=len(chosen): e.dma_start(
                    scratch[n + a][first:first + c].rearrange("t r c -> r t c"), src),
                    wait=[f"{n} part0", f"{n} part2", f"scratch {n}{a} read"], done=f"scratch {n}{a}", dma=f"out_{n}{a}")
            pg.marks[f"parts {n} written out"] = pg.marks[f"scratch {n}{a}"]

        def restack(n, a, to):
            for h in range(2):
                src = scratch[n + a].rearrange("t (d a h) c -> (t d) a h c", d=D, h=2)[:, :, h, :]
                put("sp", lambda e, i, src=src, h=h: e.dma_start(stack[to][BLK * h:BLK * h + ROWS, :, :], src),
                    wait=[f"scratch {n}{a}", f"stack {to} read", f"stack {to} copied"],
                    done=f"scratch {n}{a} read", dma=f"in_{n}{a}")
            pg.marks[f"stack {to}"] = pg.marks[f"scratch {n}{a} read"]

        def spread(n, frm):
            for g in range(GROUPS):
                pairs = slice(GROUP * g, GROUP * g + GROUP)
                for h in range(2):
                    rows = slice(BLK * h, BLK * h + ROWS)
                    put("dve", lambda e, i, rows=rows, h=h, pairs=pairs: e.tensor_copy(
                        diag[n][rows, pairs, :, BLK * h:BLK * h + BLK],
                        stack[frm][rows, pairs, :].rearrange("p a (b c) -> p a b c", c=BLK)),
                        wait=[f"stack {frm}", f"diag {n} read"], done=f"diag {n}{g}")
                pg.marks[f"stack {frm} copied"] = pg.marks[f"diag {n}{g}"]
                yield

        def values(a, n, w):
            ps, read = bank()
            heads = w.rearrange("c (a h d) -> c a h d", h=2, d=D)
            for k in range(NB):
                keys = xnT[n][:, 1 + BLK * k:1 + BLK * k + BLK]
                for h in range(2):
                    put("pe", lambda e, i, k=k, h=h, keys=keys: e.matmul(
                        ps[BLK * h:BLK * h + BLK, BLK * k:BLK * k + BLK], keys, heads[:, :, h, :], start=True, stop=True),
                        wait=[read, f"xnT{n}"], done=f"v{a}" if k == NB - 1 and h == 1 else None)
                if k == NB // 2 - 1:
                    yield
            pg.marks[f"xnT{n} read"] = pg.marks[f"v{a}"]
            for h in range(2):
                r = slice(BLK * h, BLK * h + BLK)
                put("act", lambda e, i, r=r, h=h: e.activation(
                    vals[a][r, :, :, 16 * h:16 * h + D],
                    ps[r, :].rearrange("p (b a d) -> p b a d", b=NB, a=PAIRS), ACT.Copy),
                    wait=[f"v{a}", f"vals {a} read"], done=f"vals {a}")
            pg.marks[read] = pg.marks[f"vals {a}"]
            yield

        tokens = [[C, P], [P * C, NT], [1, C]]

        def start_of(b):
            return lambda e, i: b * T * C if isinstance(i, int) else e.snap(i * (T * C) + b * T * C)

        def prepare_front(b):
            put("sp", lambda e, at: e.dma_start(xs["in"][:, :, :], bass.AP(x.tensor, at, tokens)), first=start_of(b),
                wait=["xn1"], done="x loaded", dma="x")
            yield
            yield from layernorm("1", xs["in"], "x loaded")
            for n, w in (("q", M_q), ("k", M_k)):
                ps, read = bank()
                put("pe", lambda e, i, w=w, ps=ps: e.matmul(
                    ps[:, :], w[:, :], xnT["1"][:, 1:T + 1], start=True, stop=True),
                    wait=[read, "xnT1"], done=f"{n} projected")
                split(n, "a", ps, read, f"{n} projected")
                yield

        def prepare_stacks():
            restack("q", "a", "qa")
            yield
            restack("k", "a", "k")
            yield

        def prepare_back():
            yield from spread("qa", "qa")
            yield from row_maxima(0, max_tiles)
            yield from max_rows(0)
            yield from spread("ka", "k")
            yield from row_maxima(1, max_tiles[:AHEAD])

        max_tiles = [(step, j) for step in tiles_of_keys() for j in range(0, GROUP, 2 if step[0][0] == NB // 2 else 1)]

        def row_maxima(g, tiles):
            for step, j in tiles:
                half = step[0][0] == NB // 2
                ps, read = bank()
                if half:
                    todo = [(j, NB // 2 - 1, 0), (j + 1, NB // 2 - 1, BANK // 2)]
                elif len(step) == 2:
                    i1 = NB - 1 - step[0][0]
                    todo = [(j, i1, 0), (j, step[0][0] - 1, BLK * (i1 + 1))]
                else:
                    todo = [(j, NB - 1, 0)]
                for j_, q, at in todo:
                    pr = GROUP * g + j_
                    put("pe", lambda e, i, pr=pr, q=q, at=at, ps=ps: e.matmul(
                        ps[:, at:at + BLK * (q + 1)], diag["qa"][:, pr, q, :], stack["k"][:, pr, 0:BLK * (q + 1)],
                        start=True, stop=False), wait=[read, f"diag qa{g}", "stack k"])
                    put("pe", lambda e, i, q=q, at=at, ps=ps: e.matmul(
                        ps[:, at + BLK * q:at + BLK * (q + 1)], ident_b[:, :], mask[:, :], start=False, stop=True),
                        done="raw scores")
                for j_, q, at in todo[:1] if half else todo:
                    c, n = j_ * NB + q, 2 if half else 1
                    put("dve", lambda e, i, c=c, q=q, at=at, ps=ps, n=n: e.tensor_reduce(
                        rowmax[g][:, c:c + NB * (n - 1) + 1:NB],
                        ps[:, at:at + n * BLK * (q + 1)].rearrange("p (n c) -> p n c", n=n), axis=AX.X, op=ALU.max),
                        wait=["raw scores", f"rowmax{g} read"], done=f"rowmax{g}")
                pg.marks[read] = pg.marks[f"rowmax{g}"]
                pg.marks["stack k read"] = pg.marks["diag qa read"] = pg.marks["raw scores"]
                yield

        def max_rows(g):
            mp, mr, n = mparts[g], mrest[g], GROUP * NB
            put("dve", lambda e, i: e.tensor_scalar(mp[:, 0, :], rowmax[g][:, :], -1.0, None, ALU.mult),
                wait=[f"rowmax{g}", f"max parts{g} read"], done="max part0")
            put("dve", lambda e, i: e.scalar_tensor_tensor(mr[:, :], rowmax[g][:, :], -1.0, mp[:, 0, :], ALU.mult, ALU.subtract),
                wait=["max part0"], done=f"rowmax{g} read")
            put("dve", lambda e, i: e.tensor_copy(mp[:, 1, :], mr[:, :]), wait=[f"rowmax{g} read"], done="max part1")
            put("dve", lambda e, i: e.tensor_tensor(mp[:, 2, :], mr[:, :], mp[:, 1, :], ALU.subtract),
                wait=["max part1"], done="max part2")
            yield
            ps, read = bank()
            put("pe", lambda e, i: e.matmul(ps[:, 0:P], mp[:, :, :].rearrange("p a c -> p (a c)"), ident_b[:, :],
                                            start=True, stop=True), wait=[read, "max part2"], done=f"max parts{g} read")
            put("act", lambda e, i: e.activation(mturned[g][:, :], ps[:, 0:P], ACT.Copy),
                wait=[f"max parts{g} read", f"max rows{g}"], done="max turned")
            pg.marks[read] = pg.marks["max turned"]
            for h in range(2):
                row = BLK * h + ROWS
                put("act", lambda e, i, h=h, row=row: e.dma_start(
                    stack["qa"][row:row + 3, GROUP * g:GROUP * g + GROUP, :], mturned[g][0:3 * n, BLK * h:BLK * h + BLK]),
                    wait=["max turned", "stack qa read", "stack qa copied"], done=f"max rows{g}", dma=f"max{g}")
            yield

        def scores(a, scale, g, step, u):
            q, kd = stack["q" + a], diag["k" + a]
            ready = [f"stack q{a}", f"diag k{a}{g}"] + ([f"max rows{g}"] if a == "a" else [])
            half = step[0][0] == NB // 2
            n, t = unit[0], unit[0] % 2
            unit[0] += 1
            placed = []
            for k in range(2):
                todo = ([(2 * k + z, NB // 2, z * BANK // 2) for z in range(2)] if half
                        else [(2 * u + k, blk, at) for blk, at in step])
                for j, blk, at in todo:
                    pair, width = GROUP * g + j, T - BLK * blk
                    put("pe", lambda e, i, k=k, at=at, width=width, pair=pair, blk=blk: e.matmul(
                        score[t][:, k, at:at + width], kd[:, pair, blk, :], q[:, pair, BLK * blk:T],
                        start=True, stop=False),
                        wait=[f"score{t} read", *ready])
                    put("pe", lambda e, i, k=k, at=at: e.matmul(
                        score[t][:, k, at:at + BLK], ident_b[:, :], mask_t[:, :], start=False, stop=True),
                        done=f"scores{t}")
                    placed.append((j, blk, n % NPROB, k, at))
            pg.marks[f"stack q{a} read"] = pg.marks[f"diag k{a} read"] = pg.marks[f"scores{t}"]
            pr = prob[n % NPROB]
            put("act", lambda e, i: e.activation(pr[:, :, :], score[t][:, :, :], ACT.Exp, scale=scale),
                wait=[f"scores{t}", f"prob{n % NPROB} read"], done=f"score{t} read")
            pg.marks[f"prob{n % NPROB}"] = pg.marks[f"score{t} read"]
            return placed

        def weigh(a, g, blk, tiles):
            for j, slot, k, at in tiles:
                put("pe", lambda e, i, j=j, slot=slot, k=k, at=at: e.matmul(
                    acc[32 * j:32 * j + 32, BLK * blk:T], vals[a][:, blk, GROUP * g + j, :],
                    prob[slot][:, k, at:at + T - BLK * blk], start=blk == 0, stop=blk == NB // 2),
                    wait=[f"prob{slot}", "acc read", f"vals {a}"], done=f"prob{slot} read")
                pg.marks[f"{a} summed"] = pg.marks[f"prob{slot} read"]
            if blk == NB // 2:
                put("act", lambda e, i: e.activation(outT[a][g][:, :], acc[:, :], ACT.Copy),
                    wait=[f"{a} summed", f"outT{a}{g} read"], done="acc read")
                pg.marks[f"outT{a}{g}"] = pg.marks["acc read"]

        def attend(a, scale):
            behind = []
            for g, step in [(g, step) for g in range(GROUPS) for step in tiles_of_keys()] + [(None, None)]:
                placed = []
                for u in range(1 if step and step[0][0] == NB // 2 else 2):
                    if step:
                        placed += scores(a, scale, g, step, u)
                        yield
                    if behind:
                        weigh(a, *behind.pop(0))
                        yield
                while behind:
                    weigh(a, *behind.pop(0))
                    yield
                behind = [(g, blk, [(j, *p) for j, b, *p in placed if b == blk]) for blk in sorted({p[1] for p in placed})]
            pg.marks[f"vals {a} read"] = pg.marks[f"{a} summed"]

        def normalise(a, g):
            ps, read = bank()
            src = outT[a][g]
            for k in range(NT):
                put("pe", lambda e, i, k=k: e.transpose(
                    ps[:, P * k:P * k + P], src[:, P * k:P * k + P], ident[:, :]),
                    wait=[read, f"outT{a}{g}"], done=f"outT{a}{g} read" if k == NT - 1 else None)
            heads = ps[:, :].rearrange("p (k h c) -> p k h c", k=NT, c=16)
            put("dve", lambda e, i: e.reciprocal(
                rden[a][g][:, :].rearrange("p (k h) -> p k h", k=NT), heads[:, :, :, D]),
                wait=[f"outT{a}{g} read"], done=f"rden{a}{g}")
            w = 2 * GROUP * D
            put("dve", lambda e, i: e.tensor_tensor(
                y[a][:, :, w * g:w * g + w].rearrange("p k (h d) -> p k h d", d=D), heads[:, :, :, 0:D],
                rden[a][g][:, :].rearrange("p (k h o) -> p k h o", k=NT, o=1).to_broadcast([P, NT, 2 * GROUP, D]),
                ALU.mult), wait=[f"rden{a}{g}", f"y{a} read"], done=f"y{a}")
            pg.marks[read] = pg.marks[f"y{a}"]
            yield

        def feed_forward(n, src, dst, dst_free, result):
            f = ffn
            now, before = xnT[n][:, 1:T + 1], xnT[n][:, 0:T]
            alone(lambda e, i: e.tensor_tensor(f["diff"][:, :], now, before, ALU.subtract),
                [f"xnT{n}", "mixed"], f"xnT{n} diff read")
            yield
            for k, b in enumerate(("xk", "xr")):
                put("dve", lambda e, i, k=k, b=b: e.scalar_tensor_tensor(
                    f[b][:, :], f["diff"][:, :], mu[:, 1 - k:2 - k], before, ALU.mult, ALU.add),
                    wait=[f"xnT{n} diff read", f"{b} read"], done=b)
            pg.marks["mixed"] = pg.marks[f"xnT{n} read"] = pg.marks["xr"]
            yield
            ps, read = bank()
            put("pe", lambda e, i, ps=ps: e.matmul(ps[:, :], T_k[:, :], f["xk"][:, :], start=True, stop=True),
                wait=[read, "xk"], done="xk read")
            put("act", lambda e, i, ps=ps: e.activation(f["act"][:, :], ps[:, :], ACT.Relu),
                wait=["xk read", "act read"], done="relu")
            pg.marks[read] = pg.marks["relu"]
            alone(lambda e, i: e.tensor_tensor(f["act"][:, :], f["act"][:, :], f["act"][:, :], ALU.mult),
                ["relu", "act read"], "act")
            yield
            ps, read = bank()
            for k in range(NT):
                put("pe", lambda e, i, k=k, ps=ps: e.matmul(ps[:, P * k:P * k + P], f["xr"][:, P * k:P * k + P], T_r[:, :],
                                                            start=True, stop=True),
                    wait=[read, "xr"], done="xr read" if k == NT - 1 else None)
            put("act", lambda e, i, ps=ps: e.activation(f["gate"][:, :], ps[:, :], ACT.Tanh, scale=0.5),
                wait=["xr read", "prod"], done="gate")
            pg.marks[read] = pg.marks["gate"]
            yield
            ps, read = bank()
            for k in range(NT):
                put("pe", lambda e, i, k=k, ps=ps: e.matmul(ps[:, P * k:P * k + P], f["act"][:, P * k:P * k + P], T_v[:, :],
                                                            start=True, stop=True),
                    wait=[read, "act"], done="act read" if k == NT - 1 else None)
            put("dve", lambda e, i, ps=ps: e.scalar_tensor_tensor(f["prod"][:, :], f["gate"][:, :], 1.0, ps[:, :],
                                                                  ALU.add, ALU.mult),
                wait=["act read", "gate", "prod read"], done="prod")
            pg.marks[read] = pg.marks["prod"]
            alone(lambda e, i: e.tensor_tensor(dst[:, :, :], src[:, :, :],
                                                     f["prod"][:, :].rearrange("p (k c) -> p k c", k=NT), ALU.add),
                wait=["prod", *dst_free], done=result)
            pg.marks["prod read"] = pg.marks[result]
            yield

        def middle_front(b):
            put("sp", lambda e, at: e.dma_start(xs["again"][:, :, :], bass.AP(x.tensor, at, tokens)), first=start_of(b),
                wait=["x_a"], done="x loaded again", dma="again")
            yield from normalise("a", 1)
            alone(lambda e, i: e.tensor_tensor(xs["a"][:, :, :], xs["again"][:, :, :], y["a"][:, :, :], ALU.add),
                ["ya", "x_ffn", "xn2", "x loaded again"], "x_a")
            pg.marks["ya read"] = pg.marks["x_a"]
            yield
            yield from layernorm("2", xs["a"], "x_a")
            yield from feed_forward("2", xs["a"], xs["ffn"], ["x_ffn kept", "xn3"], "x_ffn")

        def middle_back(values_last=False):
            yield from layernorm("3", xs["ffn"], "x_ffn")
            for half in range(2):
                ps, read = bank()
                for k in range(2):
                    tile = 2 * half + k
                    put("pe", lambda e, i, k=k, tile=tile, ps=ps: e.matmul(
                        ps[:, 2 * C * k:2 * C * (k + 1)], xnT["3"][:, 1 + P * tile:1 + P * (tile + 1)],
                        w_qk[:, :, :].rearrange("p a c -> p (a c)"), start=True, stop=True),
                        wait=[read, "xnT3"], done="qk projected" if k else None)
                two = slice(2 * half, 2 * half + 2)
                for to, func, free in ((qk, ACT.Square, "qk read"), (raw, ACT.Copy, "qk")):
                    put("act", lambda e, i, two=two, ps=ps, to=to, func=func: e.activation(
                        to[:, two, :, :].rearrange("p k a c -> p k (a c)"), ps[:, :].rearrange("p (k c) -> p k c", k=2), func),
                        ["qk projected", free], "raw qk")
                pg.marks[read] = pg.marks["raw qk"]
                w = 2 * 2 * HEADS
                put("dve", lambda e, i, two=two, half=half: e.tensor_reduce(
                    ssum[:, w * half:w * (half + 1)].rearrange("p (k n) -> p k n", k=2),
                    qk[:, two, :, :].rearrange("p k a (h d) -> p k (a h) d", d=D), axis=AX.X, op=ALU.add),
                    wait=["raw qk", "rnorm"], done="norms2")
                yield
            pg.marks["xnT3 read"] = pg.marks["qk projected"]
            yield from rsqrt_of_ssum()
            if not values_last:
                yield from values("b", "3", w_v[:, :])
            for half in range(2):
                two = slice(2 * half, 2 * half + 2)
                w = 2 * 2 * HEADS
                put("dve", lambda e, i, two=two, half=half: e.tensor_tensor(
                    qk[:, two, :, :].rearrange("p k a (d h) -> p (k a) h d", d=D),
                    raw[:, two, :, :].rearrange("p k a (h d) -> p (k a) h d", d=D),
                    rnorm[:, w * half:w * (half + 1)].rearrange("p (k h o) -> p k h o", k=4, o=1).to_broadcast([P, 4, HEADS, D]),
                    ALU.mult), wait=["rnorm", "raw qk", "qk read"], done="qk")
            yield
            for a, n in enumerate("qk"):
                ps, read = bank()
                for k in range(NT):
                    put("pe", lambda e, i, k=k, a=a, ps=ps: e.transpose(ps[:, P * k:P * k + P], qk[:, k, a, :], ident[:, :]),
                        wait=[read, "qk"], done=f"{n} turned" if k == NT - 1 else None)
                split(n, "b", ps, read, f"{n} turned")
                yield
            pg.marks["qk read"] = pg.marks["k turned"]
            restack("k", "b", "k")
            restack("q", "b", "qb")
            yield
            if values_last:
                yield from values("b", "3", w_v[:, :])

        def rsqrt_of_ssum():
            put("dve", lambda e, i: e.tensor_scalar(ssum[:, :], ssum[:, :], 1e-24, None, ALU.max),
                wait=["norms2"], done="norms2 kept up")
            put("dve", lambda e, i: e.tensor_scalar(rnorm[:, :].bitcast(mybir.dt.int32), ssum[:, :].bitcast(mybir.dt.int32),
                                                    -0.5, float(0x5f3759df), ALU.mult, ALU.add),
                wait=["norms2 kept up", "qk"], done="rnorm")
            for _ in range(3):
                put("dve", lambda e, i: e.scalar_tensor_tensor(step_r[:, :], rnorm[:, :], -0.5, rnorm[:, :], ALU.mult, ALU.mult),
                    wait=["rnorm"], done="rnorm step")
                put("dve", lambda e, i: e.tensor_tensor(step_r[:, :], step_r[:, :], ssum[:, :], ALU.mult),
                    wait=["rnorm step"], done="rnorm step")
                put("dve", lambda e, i: e.scalar_tensor_tensor(rnorm[:, :], step_r[:, :], 1.5, rnorm[:, :], ALU.add, ALU.mult),
                    wait=["rnorm step"], done="rnorm")
            yield

        def finish(b):
            for g in range(GROUPS):
                yield from normalise("b", g)
            ps, read = bank()
            for k in range(NT):
                put("pe", lambda e, i, k=k, ps=ps: e.transpose(ps[:, P * k:P * k + P], y["b"][:, k, :], ident[:, :]),
                    wait=[read, "yb"], done="yb read" if k == NT - 1 else None)
            put("act", lambda e, i, ps=ps: e.activation(yT[:, :], ps[:, :], ACT.Copy), wait=["yb read", "yT read"], done="yT")
            pg.marks[read] = pg.marks["yT"]
            yield
            ps, read = bank()
            for k in range(NT):
                put("pe", lambda e, i, k=k, ps=ps: e.matmul(ps[:, P * k:P * k + P], yT[:, P * k:P * k + P], w_ob[:, :],
                                                            start=True, stop=True),
                    wait=[read, "yT"], done="yT read" if k == NT - 1 else None)
            put("dve", lambda e, i, ps=ps: e.tensor_tensor(xs["b"][:, :, :], ps[:, :].rearrange("p (k c) -> p k c", k=NT),
                                                           xs["kept"][:, :, :], ALU.add),
                wait=["yT read", "x_ffn kept", "x_out", "xn4"], done="x_b")
            pg.marks[read] = pg.marks["x_b"]
            yield
            yield from layernorm("4", xs["b"], "x_b")
            yield from feed_forward("4", xs["b"], xs["out"], ["stored"], "x_out")
            put("sp", lambda e, at: e.dma_start(bass.AP(out.tensor, at, tokens), xs["out"][:, :, :]), first=start_of(b),
                wait=["x_out"], done="stored", dma="out")
            yield

        def keep():
            put("sp", lambda e, i: e.dma_start(xs["kept"][:, :, :], xs["ffn"][:, :, :]),
                wait=["x_ffn", "x_b"], done="x_ffn kept", dma="keep")
            yield

        AHEAD = len(max_tiles) - len(PLAN["row_maxima"])

        def weave(main, *sides):
            for slot in range(SLOTS):
                if main:
                    next(main, None)
                for gen, slots in sides:
                    for _ in range(slots.count(slot)):
                        next(gen, None)
            for gen in (main, *[gen for gen, _ in sides]):
                assert not [*(gen or ())], "steps are left"

        def iteration(t):
            def live(b, gen, *args):
                return [(gen(*args), PLAN[gen.__name__])] if 0 <= b < B else []

            ending = t == B
            weave(attend("a", 1.0) if t < B else None,
                  *live(t, row_maxima, 1, max_tiles[AHEAD:]), *live(t, max_rows, 1),
                  *([(rest_of_middle[0], PLAN["middle_back"])] if ending else live(t - 1, middle_back)),
                  *([] if ending else live(t - 2, finish, t - 2)), *live(t + 1, prepare_front, t + 1),
                  *([] if ending else live(t - 1, keep)), *live(t - 1, spread, "kb", "k"), *live(t, normalise, "a", 0),
                  *live(t + 1, prepare_stacks))
            sides = [*live(t, middle_front, t), *live(t + 1, values, "a", "1", M_v[:, :]), *live(t + 1, prepare_back)]
            if t == B - 1:
                rest_of_middle.append(middle_back(values_last=True))
                sides = [(sides[0][0], [2 * k for k in range(len(PLAN["middle_front"]))]),
                         (islice(rest_of_middle[0], 7), [*range(18, 32, 2)])]
            if ending:
                sides = [*live(t - 2, finish, t - 2), (keep(), [SLOTS - 1])]
            weave(attend("b", 8.0) if 0 < t <= B else None, *sides)
            ring[0] += -ring[0] % 3

        rest_of_middle = []

        pieces = []
        setup()
        for t in range(3):
            iteration(t)
        pieces.append((pg.cut(), 1, None))
        first, last = 3, B - 2
        assert last > first

        def shape(items, counts):
            return [[(s.sem.name, v - counts[s]) for s, v in waits] for waits, *_ in items]

        kept = None
        for t in range(first, last + 1):
            before, r0, u0 = pg.counts(), ring[0], unit[0]
            iteration(t)
            piece = pg.cut()
            assert (ring[0] - r0) % 3 == 0 and (unit[0] - u0) % 2 == 0 and (unit[0] - u0) % NPROB == 0
            grow = {s: n - before[s] for s, n in pg.counts().items()}
            form = {k: shape(v, before) for k, v in piece.items()}
            if kept is None:
                kept = (piece, grow, form)
            assert kept[1] == grow and kept[2] == form, "turns of the loop differ"
        pieces.append((kept[0], last - first + 1, kept[1]))
        for t in range(last + 1, B + 2):
            iteration(t)
        put("sp", lambda e, i: e.nop(), wait=["stored"])
        pieces.append((pg.cut(), 1, None))

        block = ctx.enter_context(nc.Block())

        def run(name, eng):
            for items, count, grow in pieces:
                if count == 1:
                    emit(eng, items[name])
                else:
                    with eng.Fori(0, count) as i:
                        emit(eng, items[name], i, grow)

        @block.sync
        def _(eng):
            run("sp", eng)

        @block.gpsimd
        def _(eng):
            run("pool", eng)

        @block.scalar
        def _(eng):
            run("act", eng)

        @block.vector
        def _(eng):
            run("dve", eng)

        @block.tensor
        def _(eng):
            run("pe", eng)


_NAMES = ["L0_attn_a_x", "L0_attn_a_W_dq", "L0_attn_a_W_uq", "L0_attn_a_W_dkv", "L0_attn_a_W_uk", "L0_attn_a_W_uv",
          "L0_attn_a_W_o", "L0_attn_b_Wq", "L0_attn_b_Wk", "L0_attn_b_Wv", "L0_attn_b_Wo",
          "L0_ffn_W_r", "L0_ffn_W_k", "L0_ffn_W_v", "L0_ffn_mu_r", "L0_ffn_mu_k"]


def kernel(**inputs):
    import concourse.bacc as bacc
    from concourse.bass_utils import run_bass_kernel_spmd

    nc = bacc.Bacc("TRN2", target_bir_lowering=False, num_devices=1)
    arrays, args = {}, []
    for name in _NAMES:
        a = np.ascontiguousarray(inputs[name])
        arrays["in_" + name] = a
        args.append(nc.dram_tensor("in_" + name, a.shape, mybir.dt.from_np(a.dtype), kind="ExternalInput").ap())
    shape = inputs["L0_attn_a_x"].shape
    args.append(nc.dram_tensor("out_0", shape, F32, kind="ExternalOutput").ap())
    build(nc, *args)
    r = run_bass_kernel_spmd(nc, [arrays], core_ids=[0])
    return r.results[0]["out_0"]
```
